# Optimizing a Trainium2 kernel written in Bass

```python
import numpy as np
import jax
import jax.numpy as jnp

def _softmax(x, axis=-1):
    return jax.nn.softmax(x, axis=axis)

def _gelu(x):
    return jax.nn.gelu(x, approximate=True)

def _silu(x):
    return jax.nn.silu(x)

def _sigmoid(x):
    return jax.nn.sigmoid(x)

def _layernorm(x, axis=-1, eps=1e-05):
    m = jnp.mean(x, axis=axis, keepdims=True)
    v = jnp.var(x, axis=axis, keepdims=True)
    return (x - m) / jnp.sqrt(v + eps)

def _scatter_add(tgt, idx, src, axis=0):
    return tgt.at[idx].add(src)

def _segment_sum(src, seg, n):
    return jax.ops.segment_sum(src, seg, n)
kernel_name = 'mk_hybrid_d1_jaxref_r8_bc990b'

def setup_inputs(seed: int=0):
    np.random.seed(seed)
    _w = jnp.asarray

    def _L0_attn_a_setup():
        import jax, jax.numpy as jnp
        import numpy as np
        DIM = 128
        H = 16
        D = DIM // H
        K = 64
        key = jax.random.key(seed)
        ks = jax.random.split(key, 7)
        B, S = (2, 256)
        x = jax.random.normal(ks[0], (B, S, DIM), dtype=jnp.float32)
        cantor_coords = jax.random.uniform(ks[1], (S,), dtype=jnp.float32)
        scale = 1.0 / np.sqrt(DIM)
        Wq = jax.random.normal(ks[2], (DIM, DIM), dtype=jnp.float32) * scale
        Wk = jax.random.normal(ks[3], (DIM, DIM), dtype=jnp.float32) * scale
        Wv = jax.random.normal(ks[4], (DIM, DIM), dtype=jnp.float32) * scale
        Wo = jax.random.normal(ks[5], (DIM, DIM), dtype=jnp.float32) * scale
        bo = jnp.zeros((DIM,), dtype=jnp.float32)
        return {'x': x, 'cantor_coords': cantor_coords, 'Wq': Wq, 'Wk': Wk, 'Wv': Wv, 'Wo': Wo, 'bo': bo}
    _L0_attn_a_in = _L0_attn_a_setup()

    def _L0_attn_b_setup():
        import jax, jax.numpy as jnp
        import numpy as np
        import math
        EMBED_DIM = 128
        NUM_HEADS = 16
        HEAD_DIM = EMBED_DIM // NUM_HEADS
        BLOCK_SIZE = 64
        N_GLOBAL = 8

        def _sparse_mask(seq_len: int) -> jnp.ndarray:
            idx = jnp.arange(seq_len)
            block_id = idx // BLOCK_SIZE
            local = block_id[:, None] == block_id[None, :]
            gp = np.linspace(0, seq_len - 1, min(N_GLOBAL, seq_len)).astype(np.int64)
            is_global = jnp.zeros((seq_len,), dtype=bool).at[jnp.asarray(gp)].set(True)
            return local | is_global[:, None] | is_global[None, :]
        key = jax.random.key(seed)
        ks = jax.random.split(key, 9)
        E = EMBED_DIM
        s = 0.02
        return {'x': jax.random.normal(ks[0], (1, 512, E), dtype=jnp.float32), 'Wq': jax.random.normal(ks[1], (E, E), dtype=jnp.float32) * s, 'bq': jnp.zeros((E,), dtype=jnp.float32), 'Wk': jax.random.normal(ks[2], (E, E), dtype=jnp.float32) * s, 'bk': jnp.zeros((E,), dtype=jnp.float32), 'Wv': jax.random.normal(ks[3], (E, E), dtype=jnp.float32) * s, 'bv': jnp.zeros((E,), dtype=jnp.float32), 'Wo': jax.random.normal(ks[4], (E, E), dtype=jnp.float32) * s, 'bo': jnp.zeros((E,), dtype=jnp.float32)}
    _L0_attn_b_in = _L0_attn_b_setup()

    def _L0_ffn_setup():
        import jax, jax.numpy as jnp
        import numpy as np
        TOP_K = 2
        key = jax.random.key(seed)
        k0, k1, k2, k3 = jax.random.split(key, 4)
        B, T, C, E, F = (4, 256, 128, 8, 512)
        x = jax.random.normal(k0, (B, T, C), dtype=jnp.float32)
        gate_w = jax.random.normal(k1, (C, E), dtype=jnp.float32) * 0.02
        w1 = jax.random.normal(k2, (E, C, F), dtype=jnp.float32) * 0.02
        w2 = jax.random.normal(k3, (E, F, C), dtype=jnp.float32) * 0.02
        return {'x': x, 'gate_w': gate_w, 'w1': w1, 'w2': w2}
    _L0_ffn_in = _L0_ffn_setup()
    _d = {'L0_attn_a_x': _L0_attn_a_in['x'], 'L0_attn_a_cantor_coords': _L0_attn_a_in['cantor_coords'], 'L0_attn_a_Wq': _L0_attn_a_in['Wq'], 'L0_attn_a_Wk': _L0_attn_a_in['Wk'], 'L0_attn_a_Wv': _L0_attn_a_in['Wv'], 'L0_attn_a_Wo': _L0_attn_a_in['Wo'], 'L0_attn_a_bo': _L0_attn_a_in['bo'], 'L0_attn_b_Wq': _L0_attn_b_in['Wq'], 'L0_attn_b_bq': _L0_attn_b_in['bq'], 'L0_attn_b_Wk': _L0_attn_b_in['Wk'], 'L0_attn_b_bk': _L0_attn_b_in['bk'], 'L0_attn_b_Wv': _L0_attn_b_in['Wv'], 'L0_attn_b_bv': _L0_attn_b_in['bv'], 'L0_attn_b_Wo': _L0_attn_b_in['Wo'], 'L0_attn_b_bo': _L0_attn_b_in['bo'], 'L0_ffn_gate_w': _L0_ffn_in['gate_w'], 'L0_ffn_w1': _L0_ffn_in['w1'], 'L0_ffn_w2': _L0_ffn_in['w2']}
    _x0 = _d['L0_attn_a_x']
    _d['L0_attn_a_x'] = jax.random.normal(jax.random.fold_in(jax.random.key(seed), 1), (4, 1024, 128), dtype=_x0.dtype)
    del _x0
    return _d

def reference(L0_attn_a_x, L0_attn_a_cantor_coords, L0_attn_a_Wq, L0_attn_a_Wk, L0_attn_a_Wv, L0_attn_a_Wo, L0_attn_a_bo, L0_attn_b_Wq, L0_attn_b_bq, L0_attn_b_Wk, L0_attn_b_bk, L0_attn_b_Wv, L0_attn_b_bv, L0_attn_b_Wo, L0_attn_b_bo, L0_ffn_gate_w, L0_ffn_w1, L0_ffn_w2):

    def _L0_attn_a_ref(x, cantor_coords, Wq, Wk, Wv, Wo, bo):
        import jax, jax.numpy as jnp
        import numpy as np
        DIM = 128
        H = 16
        D = DIM // H
        K = 64
        B, S, Dim = x.shape
        q = jnp.einsum('bsd,ed->bse', x, Wq).reshape(B, S, H, D)
        k = jnp.einsum('bsd,ed->bse', x, Wk).reshape(B, S, H, D)
        v = jnp.einsum('bsd,ed->bse', x, Wv).reshape(B, S, H, D)
        idx = jnp.arange(S)[:, None]
        off = jnp.arange(-K // 2, K // 2)[None, :]
        routes = jnp.clip(idx + off, 0, S - 1)
        kg = k[:, routes]
        vg = v[:, routes]
        scores = jnp.einsum('bshd,bskhd->bshk', q, kg) / np.sqrt(D)
        attn = jax.nn.softmax(scores, axis=-1)
        out = jnp.einsum('bshk,bskhd->bshd', attn, vg).reshape(B, S, Dim)
        return jnp.einsum('bsd,ed->bse', out, Wo) + bo

    def _L0_attn_b_ref(x, Wq, bq, Wk, bk, Wv, bv, Wo, bo):
        import jax, jax.numpy as jnp
        import numpy as np
        import math
        EMBED_DIM = 128
        NUM_HEADS = 16
        HEAD_DIM = EMBED_DIM // NUM_HEADS
        BLOCK_SIZE = 64
        N_GLOBAL = 8

        def _sparse_mask(seq_len: int) -> jnp.ndarray:
            idx = jnp.arange(seq_len)
            block_id = idx // BLOCK_SIZE
            local = block_id[:, None] == block_id[None, :]
            gp = np.linspace(0, seq_len - 1, min(N_GLOBAL, seq_len)).astype(np.int64)
            is_global = jnp.zeros((seq_len,), dtype=bool).at[jnp.asarray(gp)].set(True)
            return local | is_global[:, None] | is_global[None, :]
        B, S, E = x.shape
        H, D = (NUM_HEADS, HEAD_DIM)
        mask = _sparse_mask(S)

        def split_heads(y):
            return y.reshape(B, S, H, D).transpose(0, 2, 1, 3)
        q = split_heads(x @ Wq + bq)
        k = split_heads(x @ Wk + bk)
        v = split_heads(x @ Wv + bv)
        scale = math.sqrt(D)
        scores = jnp.einsum('bhqd,bhkd->bhqk', q, k) / scale
        scores = jnp.where(mask[None, None], scores, -jnp.inf)
        attn = jax.nn.softmax(scores, axis=-1)
        out = jnp.einsum('bhqk,bhkd->bhqd', attn, v)
        out = out.transpose(0, 2, 1, 3).reshape(B, S, E)
        return out @ Wo + bo

    def _L0_ffn_ref(x, gate_w, w1, w2):
        import jax, jax.numpy as jnp
        import numpy as np
        TOP_K = 2
        E = gate_w.shape[-1]
        probs = jax.nn.softmax(x @ gate_w, axis=-1)
        topw, topi = jax.lax.top_k(probs, TOP_K)
        topw = topw / topw.sum(axis=-1, keepdims=True)
        combine = (jax.nn.one_hot(topi, E, dtype=x.dtype) * topw[..., None]).sum(axis=-2)

        def body(acc, params):
            w1_i, w2_i, cw = params
            h = jax.nn.gelu(x @ w1_i, approximate=False)
            return (acc + cw[..., None] * (h @ w2_i), None)
        acc0 = jnp.zeros_like(x)
        out, _ = jax.lax.scan(body, acc0, (w1, w2, jnp.moveaxis(combine, -1, 0)))
        return out
    x = L0_attn_a_x
    x = x + _L0_attn_a_ref(_layernorm(x, axis=-1), L0_attn_a_cantor_coords, L0_attn_a_Wq, L0_attn_a_Wk, L0_attn_a_Wv, L0_attn_a_Wo, L0_attn_a_bo)
    x = x + _L0_ffn_ref(_layernorm(x, axis=-1), L0_ffn_gate_w, L0_ffn_w1, L0_ffn_w2)
    x = x + _L0_attn_b_ref(_layernorm(x, axis=-1), L0_attn_b_Wq, L0_attn_b_bq, L0_attn_b_Wk, L0_attn_b_bk, L0_attn_b_Wv, L0_attn_b_bv, L0_attn_b_Wo, L0_attn_b_bo)
    x = x + _L0_ffn_ref(_layernorm(x, axis=-1), L0_ffn_gate_w, L0_ffn_w1, L0_ffn_w2)
    return x

_drawn_inputs = setup_inputs


def setup_inputs(seed=0):
    import zlib

    import numpy as np

    out = dict(_drawn_inputs(seed))
    spreads = {'L0_attn_a_bo': (0.0, 0.1),
     'L0_attn_b_bq': (0.0, 0.8),
     'L0_attn_b_bk': (0.0, 0.8),
     'L0_attn_b_bv': (0.0, 0.334),
     'L0_attn_b_bo': (0.0, 0.1)}
    factors = {'L0_attn_b_Wq': 8.0, 'L0_attn_b_Wk': 8.0, 'L0_attn_b_Wv': 6.452}
    for name, (base, spread) in spreads.items():
        noise = np.random.default_rng([zlib.crc32(name.encode()), seed]).standard_normal(out[name].shape)
        drawn = base * np.exp(spread * noise) if base else spread * noise
        out[name] = jnp.asarray(drawn.astype(out[name].dtype))
    for name, factor in factors.items():
        out[name] = (out[name] * factor).astype(out[name].dtype)
    return out
```

```python
from contextlib import ExitStack

import numpy as np

import concourse.bass as bass
from concourse import mybir

F32 = mybir.dt.float32
F32R = mybir.dt.float32r
BF16 = mybir.dt.bfloat16
U32 = mybir.dt.uint32
ALU = mybir.AluOpType
ACT = mybir.ActivationFunctionType
AX_X = mybir.AxisListType.X

P = 128
B, S, C = 4, 1024, 128
H, D = 16, 8
J, G = 4, 4
ROWS = P // J
TB = S // P
TT = B * TB
QB = 64
NBLK = S // QB
WIN = 64
PAD = WIN // 2
EXT_A = S + 2 * PAD
KEYS_A = 2 * QB
SPAN_A = P + 2 * PAD
NG = 8
KEYS_B = QB + NG
EXT_B = NBLK * KEYS_B
SPAN_B = 2 * KEYS_B
GLOBALS = [int(v) for v in np.linspace(0, S - 1, NG).astype(np.int64)]
E, F = 8, 512
FC = F // P
SCALE = float(D) ** -0.5
EPS = 1e-5
MASKED = -1e30


def constants():
    q, k = np.arange(P)[:, None], np.arange(SPAN_A)[None, :]
    a_max = np.where((k >= q) & (k < q + WIN), 0.0, MASKED)
    q, k = (np.arange(P) % QB)[:, None], np.arange(KEYS_A)[None, :]
    a_exp = np.where((k >= q) & (k < q + WIN), 0.0, MASKED)
    q, k = (np.arange(P) // QB)[:, None], (np.arange(SPAN_B) // KEYS_B)[None, :]
    b_max = np.where(q == k, 0.0, MASKED)
    b_exp = np.zeros((P, TB, KEYS_B))
    for i, pos in enumerate(GLOBALS):
        blk = pos // QB
        b_exp[(blk % 2) * QB:(blk % 2 + 1) * QB, blk // 2, QB + i] = MASKED
    masks = np.concatenate([a_max, a_exp, b_max, b_exp.reshape(P, -1), np.eye(P)], axis=1)
    row = np.arange(P) % ROWS
    term, d = row // D, row % D
    k_lo, q_lo, spare = term == 2, term == 1, term == 3
    cols = np.zeros((P, 8), np.float32)
    cols[:, 0] = np.where(spare, 0, np.where(k_lo, -1, 1))
    cols[:, 1] = k_lo
    cols[:, 2] = spare & (d == 0)
    cols[:, 3] = np.where(spare, 0, np.where(q_lo, -1, 1))
    cols[:, 4] = q_lo
    heads = np.zeros((P, H), np.float32)
    heads[np.arange(P), 4 * ((np.arange(P) // D) % G) + np.arange(P) // ROWS] = 1
    stack = np.zeros((P, G), np.float32)
    stack[np.arange(P), (np.arange(P) // D) % G] = 1
    experts = np.tile(np.arange(E, dtype=np.float32), (P, 1))
    table = np.concatenate([np.eye(P, dtype=np.float32), cols, heads, stack, experts], axis=1)
    return masks.astype(np.float32), np.ascontiguousarray(table.astype(np.float32))


class Token:

    def __init__(self, sem_name, amount):
        self.sem_name, self.amount, self.waited, self.value = sem_name, amount, False, None


class Queues:

    ENGINES = ("sync", "tensor", "vector", "scalar", "gpsimd")

    def __init__(self):
        self.steps = {e: [] for e in self.ENGINES}

    def add(self, engine, stage, after, amount, instruction, *operands, **options):
        token = Token(f"{engine}_{stage}", amount)
        self.steps[engine].append((instruction, operands, options, after, token))
        return token

    def play(self, nc, ctx, block):
        for steps in self.steps.values():
            for _, _, _, after, _ in steps:
                for token in after:
                    if token is not None:
                        token.waited = True
        sems, count = {}, {}
        for engine in self.ENGINES:
            for *_, token in self.steps[engine]:
                if token.waited:
                    name = token.sem_name
                    if name not in sems:
                        sems[name] = ctx.enter_context(nc.semaphore(name))
                    count[name] = count.get(name, 0) + token.amount
                    token.value = count[name]

        def run(engine):
            def body(eng):
                reached = {}
                for instruction, operands, options, after, token in self.steps[engine]:
                    for t in after:
                        if t is not None and reached.get(t.sem_name, 0) < t.value:
                            eng.wait_ge(sems[t.sem_name], t.value)
                            reached[t.sem_name] = t.value
                    ins = instruction(*operands, **options)
                    if token.waited:
                        ins.then_inc(sems[token.sem_name], token.amount)
            return body

        block.sync(run("sync"))
        block.tensor(run("tensor"))
        block.vector(run("vector"))
        block.scalar(run("scalar"))
        block.gpsimd(run("gpsimd"))


def build(nc, x_in, w_a, bo_a, w_b, b_b, b_cols_in, gate_w, w1, w2, masks_in, table_in, out):
    Q = Queues()

    def pe(stage, after, instruction, *operands, **options):
        return Q.add("tensor", stage, after, 1, instruction, *operands, **options)

    def dve(stage, after, instruction, *operands, **options):
        return Q.add("vector", stage, after, 1, instruction, *operands, **options)

    def act(stage, after, instruction, *operands, **options):
        return Q.add("scalar", stage, after, 1, instruction, *operands, **options)

    def pool(stage, after, instruction, *operands, **options):
        return Q.add("gpsimd", stage, after, 1, instruction, *operands, **options)

    n_dma = [0]

    def dma(name, dst, src, *after):
        n_dma[0] += 1
        return Q.add("sync", f"{name}_{n_dma[0]}", after, 16, nc.sync.dma_start, dst, src)

    with ExitStack() as ctx:
        def sb(name, shape, dt=F32):
            return ctx.enter_context(nc.sbuf_tensor(name, shape, dt))

        x = sb("x", [P, TT, C])
        xn = sb("xn", [P, TB, C])
        ext = sb("ext", [P, EXT_B])
        kst = sb("kst", [P, G, EXT_B], F32R)
        qst = sb("qst", [P, G, S], F32R)
        rounded = sb("rounded", [P, 2, 512], F32)
        shifted = sb("shifted", [P, 2, 512], F32)
        kpl = sb("kpl", [P, S])
        v = sb("v", [P, NBLK, C])
        pt = sb("pt", [P, 2, J, G * P])
        rden = sb("rden", [P, 2, G * P])
        on = sb("on", [P, TB, G * P])
        mx = sb("mx", [P, J, G, TB])
        mxT = sb("mxT", [P, P], F32R)
        w_attn = [sb(f"w_attn{l}", [P, 4, C]) for l in range(2)]
        w_stack = [sb(f"w_stack{l}", [P, 2, G, P]) for l in range(2)]
        w_out = [sb(f"w_out{l}", [P, G, C]) for l in range(2)]
        bo_row = sb("bo_row", [1, 2, C])
        b_nat = sb("b_nat", [P, 4, C])
        b_cols = sb("b_cols", [P, 2, 1 + G])
        gbias = sb("gbias", [P, 2, 2, G])
        gate = sb("gate", [P, E])
        w1_sb = sb("w1_sb", [P, E, F])
        w2_sb = sb("w2_sb", [P, E, FC, C])
        masks = sb("masks", [P, SPAN_A + KEYS_A + SPAN_B + TB * KEYS_B + P], BF16)
        table = sb("table", [P, P + 8 + H + G + E])
        ones = sb("ones", [P, P])
        power = sb("power", [P, TB])
        stats = sb("stats", [P, TB, 6])
        mv = sb("mv", [P, TB, 2])
        veps = sb("veps", [P, TB])
        rstd = sb("rstd", [P, TB])
        gq = sb("gq", [P, NG])
        gbd = sb("gbd", [P, H, NG])
        gp = sb("gp", [P, S])
        gs = sb("gs", [P, 4])
        gpT = sb("gpT", [QB, NBLK, P])
        gsel = sb("gsel", [P, H, NG])
        gout = sb("gout", [P, NG])
        xnT = sb("xnT", [P, S])
        hT = sb("hT", [P, 2, FC, 512])
        logits = sb("logits", [P, TB, E])
        top = sb("top", [P, TB, 8])
        topi = sb("topi", [P, TB, 8], U32)
        topf = sb("topf", [P, TB, 2])
        wdif = sb("wdif", [P, TB, 1])
        wexp = sb("wexp", [P, TB, 1])
        wsum = sb("wsum", [P, TB, 1])
        wtop = sb("wtop", [P, 2, TB, 1])
        hot = sb("hot", [P, 2, TB, E])
        cw = sb("cw", [P, TB, E])

        bank = [ctx.enter_context(nc.psum_tensor(f"bank{i}", [P, 512], F32)) for i in range(8)]
        freed = [[] for _ in range(8)]

        at = 0
        mask_ap = {}
        for name, n in (("a_max", SPAN_A), ("a_exp", KEYS_A), ("b_max", SPAN_B), ("b_exp", TB * KEYS_B), ("eye", P)):
            mask_ap[name] = masks[:, at:at + n]
            at += n
        eye16 = mask_ap["eye"]
        eye = table[:, 0:P]
        kcol = [table[:, P + i:P + i + 1] for i in range(3)]
        qcol = [table[:, P + 3 + i:P + 4 + i] for i in range(2)]
        head_of = table[:, P + 8:P + 8 + H]
        stack_of = table[:, P + 8 + H:P + 8 + H + G]
        iota_e = table[:, P + 8 + H + G:]

        x_dram = x_in.rearrange("b (t p) c -> b p t c", p=P)
        out_dram = out.rearrange("b (t p) c -> b p t c", p=P)
        got_x = [dma("x", x[:, b * TB:(b + 1) * TB, :], x_dram[b]) for b in range(1)]
        got_table = dma("table", table[:], table_in)
        got_w = [dma("wa", w_attn[0][:], w_a.rearrange("m c e -> c m e"))]
        n_mask = masks.shape[1]
        staged = pt[:, 0].rearrange("p j n -> p (j n)")[:, 0:n_mask]
        masks_landed = dma("masks", staged, masks_in)
        got_x += [dma("x", x[:, b * TB:(b + 1) * TB, :], x_dram[b]) for b in range(1, B)]
        got_bo = [dma("bo", bo_row[0:1, 0, :], bo_a)]
        got_gate = dma("gate", gate[:], gate_w)
        got_w1 = dma("w1", w1_sb[:], w1.rearrange("e c f -> c e f"))
        got_w2 = dma("w2", w2_sb[:], w2.rearrange("e (k f) c -> f e k c", f=P))
        got_w.append(dma("wb", w_attn[1][:], w_b.rearrange("m c e -> c m e")))
        got_bo.append(dma("bo", bo_row[0:1, 1, :], b_b[3:4, :]))
        got_bias = dma("bv", b_nat[:, 2, :], b_b[2:3, :].broadcast_to([P, C]))
        got_cols = dma("bcols", b_cols[:], b_cols_in)

        zero_cols = dve("zero", [], nc.vector.memset,
            gbias[:], 0.0)
        ones_set = dve("ones", [], nc.vector.memset,
            ones[:], 1.0)
        power_set = dve("power", [], nc.vector.memset,
            power[:], -0.5)
        got_masks = dve("masks", [masks_landed], nc.vector.tensor_copy, masks[:], staged)
        stack_set, out_set = [], []
        for l in range(2):
            for m in range(2):
                for g in range(G):
                    src = w_attn[l][:, m, :].rearrange("p (j g d) -> p j g d", j=J, g=G)[:, :, g, :]
                    for term in range(4):
                        dst = w_stack[l][:, m, g, :].rearrange("p (j t d) -> p j t d", j=J, t=4)[:, :, term, :]
                        last = pool("stack", [got_w[l]], nc.gpsimd.tensor_copy,
                            dst, src)
            stack_set.append(last)
            for g in range(G):
                last = pool("wout", [got_w[l], got_table], nc.gpsimd.tensor_scalar,
                    w_out[l][:, g, :], w_attn[l][:, 3, :], stack_of[:, g:g + 1], None, ALU.mult)
            out_set.append(last)

        x_ready = [[got_x[b]] for b in range(B)]

        def layer_norm(b):
            tiles = range(TB)
            for t in tiles:
                st = dve("bn", [*x_ready[b]], nc.vector.bn_stats,
                    stats[:, t, :], x[:, b * TB + t, :])
            for t in tiles:
                ag = dve("agg", [st], nc.vector.bn_aggr,
                    mv[:, t, :], stats[:, t, :])
            ve = dve("veps", [ag, *rstd_read], nc.vector.tensor_scalar,
                veps[:], mv[:, :, 1], EPS, None, ALU.add)
            rs = pool("rstd", [ve, power_set], nc.gpsimd.tensor_tensor,
                rstd[:], veps[:], power[:], ALU.pow)
            done = []
            for t in tiles:
                done.append(dve("norm", [rs, *xn_read], nc.vector.tensor_scalar,
                    xn[:, t, :], x[:, b * TB + t, :], mv[:, t, 0:1], rstd[:, t:t + 1], ALU.subtract, ALU.mult))
            rstd_read[:] = [done[-1]]
            return done

        rstd_read, xn_read = [], []

        def transposed(normed, dst_of, *dst_free):
            copies = []
            for c in range(TB // 4):
                bk = 6 + c % 2
                for t in range(4 * c, 4 * c + 4):
                    tr = pe("xT", [normed[t], got_table, *freed[bk]], nc.tensor.transpose,
                        bank[bk][:, (t % 4) * P:(t % 4 + 1) * P], xn[:, t, :], eye)
                copies.append(act("xT", [tr, *dst_free], nc.scalar.copy,
                    dst_of(c), bank[bk][:].rearrange("p (n q) -> p n q", q=QB)))
                freed[bk] = [copies[-1]]
            xn_read[:] = [tr]
            return copies

        ring = {"rounded": [None, None], "n": 0}
        last_use = {"ext": [], "kst": [], "qst": [], "v": [], "on": [], "mxT": [], "xnT": [], "pt": [[got_masks], []],
                    "rden": [[], []], "hT": [[], []], "kpl": [], "cw": []}

        def attention(l, b):
            keys, ext_n, span = ((KEYS_A, EXT_A, SPAN_A), (KEYS_B, EXT_B, SPAN_B))[l]
            step = (QB, KEYS_B)[l]
            normed = layer_norm(b)
            if l == 0:
                body = lambda c: ext[:, PAD + 512 * c:PAD + 512 * c + 512].rearrange("p (n q) -> p n q", q=QB)
            else:
                body = lambda c: ext[:, 0:EXT_B].rearrange("p (n k) -> p n k", k=KEYS_B)[:, 8 * c:8 * c + 8, 0:QB]
            copies = transposed(normed, body, *last_use["ext"])
            if l == 0:
                e1 = dve("edge", [copies[0]], nc.vector.tensor_copy,
                    ext[:, 0:PAD], ext[:, PAD:PAD + 1].broadcast_to([P, PAD]))
                e2 = dve("edge", [copies[1]], nc.vector.tensor_copy,
                    ext[:, PAD + S:EXT_A], ext[:, PAD + S - 1:PAD + S].broadcast_to([P, PAD]))
                ext_full = [*copies, e1, e2]
            else:
                ext_full = list(copies)
                blocks = ext[:, 0:EXT_B].rearrange("p (n k) -> p n k", k=KEYS_B)
                for i, pos in enumerate(GLOBALS):
                    src = (pos // QB) * KEYS_B + pos % QB
                    ext_full.append(dve("edge", [copies[pos // 512]], nc.vector.tensor_copy,
                        blocks[:, :, QB + i], ext[:, src:src + 1].broadcast_to([P, NBLK])))
            own = 512 if l == 0 else 8 * KEYS_B

            def project(m, g, lo, n, view, dst):
                i = ring["n"]
                ring["n"] += 1
                bk, r = 4 + i % 2, i % 2
                sign, part = ((qcol[0], qcol[1]), (kcol[0], kcol[1]))[m]
                mm = pe("proj", [stack_set[l], *ext_full, *freed[bk]], nc.tensor.matmul,
                    bank[bk][:, 0:n], w_stack[l][:, m, g, :], view, start=True, stop=True)
                off = gbias[:, l, m, g:g + 1]
                rd = act("round", [mm, bias_set, ring["rounded"][r]], nc.scalar.activation,
                    rounded[:, r, 0:n].bitcast(F32R), bank[bk][:, 0:n], ACT.Identity, bias=off, scale=sign)
                if l == 0:
                    sp = dve("split", [rd, *last_use[("qst", "kst")[m]]], nc.vector.scalar_tensor_tensor,
                        out=dst, in0=bank[bk][:, 0:n], scalar=part, in1=rounded[:, r, 0:n], op0=ALU.mult,
                        op1=ALU.add)
                    freed[bk] = [rd, sp]
                else:
                    sh = dve("shift", [rd, bias_set], nc.vector.tensor_scalar,
                        shifted[:, r, 0:n], bank[bk][:, 0:n], b_cols[:, m, 1 + g:2 + g], part, ALU.add, ALU.mult)
                    sp = dve("split", [sh, *last_use[("qst", "kst")[m]]], nc.vector.tensor_tensor,
                        dst, shifted[:, r, 0:n], rounded[:, r, 0:n], ALU.add)
                    freed[bk] = [rd, sh]
                ring["rounded"][r] = sp
                return sp

            for g in range(G):
                for c in range(S // 512):
                    view = body(c) if l else ext[:, PAD + 512 * c:PAD + 512 * c + 512]
                    q_split = project(0, g, 512 * c, 512, view, qst[:, g, 512 * c:512 * c + 512])
                for lo in range(0, ext_n, 512):
                    n = min(512, ext_n - lo)
                    k_split = project(1, g, lo, n, ext[:, lo:lo + n], kst[:, g, lo:lo + n])
            for c in range(NBLK // 4):
                bk = 6 + c % 2
                for i in range(4):
                    blk = 4 * c + i
                    mm = pe("v", [got_w[l], *ext_full, *freed[bk]], nc.tensor.matmul,
                        bank[bk][0:keys, i * C:(i + 1) * C], ext[:, blk * step:blk * step + keys],
                        w_attn[l][:, 2, :], start=i == 0, stop=i == 3, skip_group_check=True)
                src = bank[bk][0:keys, :].rearrange("p (n c) -> p n c", c=C)
                if l == 0:
                    v_set = act("v", [mm, *last_use["v"]], nc.scalar.copy,
                        v[0:keys, 4 * c:4 * c + 4, :], src)
                else:
                    v_set = dve("v", [mm, got_bias, *last_use["v"]], nc.vector.tensor_tensor,
                        v[0:keys, 4 * c:4 * c + 4, :], src, b_nat[0:keys, 2:3, :].broadcast_to([keys, 4, C]),
                        ALU.add)
                freed[bk] = [v_set]
            last_use["ext"] = [mm]
            g_done = global_queries(b, ext_full, v_set) if l else []

            mask = mask_ap[("a_max", "b_max")[l]]
            for t in range(TB):
                for gp2 in range(G // 2):
                    for j in range(J):
                        bk = j + 4 * gp2
                        pe("mmask", [got_masks, *freed[bk]], nc.tensor.matmul,
                            bank[bk][:, 0:2 * span], eye16,
                            mask.rearrange("p (o k) -> p o k", o=1).broadcast_to([P, 2, span]), start=True,
                            stop=False, skip_group_check=True)
                    for i in range(2):
                        g = 2 * gp2 + i
                        first = t * P if l == 0 else 2 * t * KEYS_B
                        for j in range(J):
                            bk, r = j + 4 * gp2, slice(j * ROWS, (j + 1) * ROWS)
                            mm = pe("mscore", [q_split, k_split], nc.tensor.matmul,
                                bank[bk][:, i * span:(i + 1) * span], qst[r, g, t * P:(t + 1) * P],
                                kst[r, g, first:first + span], start=False, stop=i == 1, skip_group_check=True,
                                tile_position=(r.start, 0))
                            if i == 1:
                                md = dve("max", [mm], nc.vector.reduce_max,
                                    mx[:, j, 2 * gp2:2 * gp2 + 2, t],
                                    bank[bk][:, 0:2 * span].rearrange("p (g k) -> p g k", g=2), AX_X)
                                freed[bk] = [md]
            tr = pe("mT", [md, *freed[7]], nc.tensor.transpose,
                bank[7][:, 0:P], mx[:].rearrange("p j g t -> p (j g t)"), eye)
            neg = dve("neg", [tr, *last_use["mxT"]], nc.vector.tensor_scalar,
                mxT[:], bank[7][:, 0:P], -1.0, None, ALU.mult)
            freed[7] = [neg]
            rows = [dma("mrow", qst[j * ROWS + 3 * D:j * ROWS + 3 * D + 1, :, :].rearrange("o g s -> o (g s)")
                        .rearrange("o (r q) -> o r q", q=P).bitcast(F32), mxT[32 * j:32 * j + 32, :].bitcast(F32),
                        neg, mm)
                    for j in range(J)]
            last_use["mxT"] = rows

            for t in range(TB):
                r2 = t % 2
                mask = mask_ap["a_exp"] if l == 0 else mask_ap["b_exp"][:, t * KEYS_B:(t + 1) * KEYS_B]
                for j in range(J):
                    pe("emask", [*freed[j]], nc.tensor.matmul,
                        bank[j][0:keys, :], mask, eye16.rearrange("p (o q) -> p o q", o=1).broadcast_to([P, G, P]),
                        start=True, stop=False, skip_group_check=True)
                exps = []
                for g in range(G):
                    for h in range(2):
                        blk = 2 * t + h
                        for j in range(J):
                            r = slice(j * ROWS, (j + 1) * ROWS)
                            mm = pe("escore", [*rows], nc.tensor.matmul,
                                bank[j][0:keys, g * P + h * QB:g * P + (h + 1) * QB],
                                kst[r, g, blk * step:blk * step + keys], qst[r, g, blk * QB:(blk + 1) * QB],
                                start=False, stop=g == G - 1 and h == 1, skip_group_check=True,
                                tile_position=(r.start, 0))
                            if g == G - 1 and h == 1:
                                ex = act("exp", [mm, *last_use["pt"][r2]], nc.scalar.activation,
                                    pt[0:keys, r2, j, :], bank[j][0:keys, :], ACT.Exp, scale=SCALE)
                                exps.append(ex)
                                freed[j] = [ex]
                num, den = (bank[4], bank[5]) if r2 == 0 else (bank[6], bank[7])
                nb, db = (4, 5) if r2 == 0 else (6, 7)
                for h in range(2):
                    for j in range(J):
                        c = slice(j * ROWS, (j + 1) * ROWS)
                        pcol = pt[0:keys, r2, j, :].rearrange("p (g b q) -> p g b q", g=G, b=2)[:, :, h, :]
                        ncol = num[c, :].rearrange("p (g b q) -> p g b q", g=G, b=2)[:, :, h, :]
                        dcol = den[c, :].rearrange("p (g b q) -> p g b q", g=G, b=2)[:, :, h, :]
                        pe("pv", [exps[j], v_set, *freed[nb]], nc.tensor.matmul,
                            ncol, v[0:keys, 2 * t + h, c], pcol, start=h == 0, stop=h == 1, skip_group_check=True,
                            tile_position=(0, c.start))
                        mm = pe("den", [ones_set, *freed[db]], nc.tensor.matmul,
                            dcol, ones[0:keys, c], pcol, start=h == 0, stop=h == 1, skip_group_check=True,
                            tile_position=(0, c.start))
                last_use["pt"][r2] = [mm]
                rc = dve("rden", [mm], nc.vector.reciprocal,
                    rden[:, r2, :], den[:])
                on_set = dve("on", [rc, *last_use["on"]], nc.vector.tensor_tensor,
                    on[:, t, :], num[:], rden[:, r2, :], ALU.mult)
                freed[nb], freed[db] = [on_set], [rc]
                for i, pos in enumerate(GLOBALS if l else []):
                    if pos // P == t:
                        on_set = dve("gput", [on_set, *g_done], nc.vector.tensor_copy,
                            on[:, t, :].rearrange("p (g q) -> p g q", g=G)[:, :, pos % P],
                            gout[:, i:i + 1].broadcast_to([P, G]))
                for g in range(G):
                    pe("wo", [on_set, out_set[l]], nc.tensor.matmul,
                        bank[nb][:, 0:C], on[:, t, g * P:(g + 1) * P], w_out[l][:, g, :], start=g == 0, stop=False)
                wo = pe("wo", [got_bo[l]], nc.tensor.matmul,
                    bank[nb][:, 0:C], ones[0:1, :], bo_row[0:1, l, :], start=False, stop=True)
                rs = dve("resid", [wo], nc.vector.tensor_tensor,
                    x[:, b * TB + t, :], x[:, b * TB + t, :], bank[nb][:, 0:C], ALU.add)
                freed[nb] = [rs]
            last_use["kst"] = last_use["qst"] = last_use["v"] = [mm]
            last_use["on"] = [wo]
            x_ready[b] = [rs]

        def global_queries(b, ext_full, v_set):
            for c in range(S // 512):
                bk = 4 + c % 2
                src = ext[:, 0:EXT_B].rearrange("p (n k) -> p n k", k=KEYS_B)[:, 8 * c:8 * c + 8, 0:QB]
                mm = pe("gk", [*freed[bk]], nc.tensor.matmul,
                    bank[bk][:], w_attn[1][:, 1, :], src, start=True, stop=True)
                kp = act("gk", [mm, bias_set], nc.scalar.activation,
                    kpl[:, 512 * c:512 * c + 512], bank[bk][:], ACT.Identity, bias=b_cols[:, 1, 0:1])
                freed[bk] = [kp]
            mm = pe("gq", [*freed[6]], nc.tensor.matmul,
                bank[6][:, 0:NG], w_attn[1][:, 0, :], ext[:, QB:KEYS_B], start=True, stop=True)
            gqd = dve("gq", [mm, bias_set], nc.vector.tensor_scalar,
                gq[:], bank[6][:, 0:NG], b_cols[:, 0, 0:1], None, ALU.add)
            freed[6] = [gqd]
            bd = dve("gbd", [gqd], nc.vector.tensor_tensor,
                gbd[:], gq[:].rearrange("p (o n) -> p o n", o=1).broadcast_to([P, H, NG]),
                head_of.rearrange("p (h o) -> p h o", o=1).broadcast_to([P, H, NG]), ALU.mult)
            gbd2 = gbd[:].rearrange("p h n -> p (h n)")
            for c in range(2):
                mm = pe("gs", [bd, kp, *freed[c]], nc.tensor.matmul,
                    bank[c][:], gbd2, kpl[:, 512 * c:512 * c + 512], start=True, stop=True)
                g1 = dve("gmax", [mm], nc.vector.reduce_max,
                    gs[:, c:c + 1], bank[c][:], AX_X)
            g2 = dve("gmax", [g1], nc.vector.tensor_tensor,
                gs[:, 2:3], gs[:, 0:1], gs[:, 1:2], ALU.max)
            g3 = dve("gmax", [g2], nc.vector.tensor_scalar,
                gs[:, 3:4], gs[:, 2:3], -SCALE, None, ALU.mult)
            for c in range(2):
                ex = act("gexp", [g3], nc.scalar.activation,
                    gp[:, 512 * c:512 * c + 512], bank[c][:], ACT.Exp, bias=gs[:, 3:4], scale=SCALE)
                freed[c] = [ex]
            g4 = dve("gsum", [ex], nc.vector.reduce_sum,
                gs[:, 0:1], gp[:], AX_X)
            g5 = dve("gsum", [g4], nc.vector.reciprocal,
                gs[:, 1:2], gs[:, 0:1])
            g6 = dve("gnorm", [g5], nc.vector.tensor_scalar,
                gp[:], gp[:], gs[:, 1:2], None, ALU.mult)
            for c in range(4):
                for i in range(4):
                    n = 4 * c + i
                    tr = pe("gT", [g6, *freed[c]], nc.tensor.transpose,
                        bank[c][0:QB, i * P:(i + 1) * P], gp[:, n * QB:(n + 1) * QB], eye)
                cp = act("gT", [tr], nc.scalar.copy,
                    gpT[:, 4 * c:4 * c + 4, :], bank[c][0:QB, :] .rearrange("p (n q) -> p n q", q=P))
                freed[c] = [cp]
            for n in range(NBLK):
                mm = pe("gpv", [cp, v_set, *freed[6]], nc.tensor.matmul,
                    bank[6][:, 0:P], v[0:QB, n, :], gpT[:, n, :], start=n == 0, stop=n == NBLK - 1)
            sl = dve("gsel", [mm], nc.vector.tensor_tensor,
                gsel[:], bank[6][:, 0:P].rearrange("p (h n) -> p h n", h=H),
                head_of.rearrange("p (h o) -> p h o", o=1).broadcast_to([P, H, NG]), ALU.mult)
            freed[6] = [sl]
            return [dve("gout", [sl], nc.vector.reduce_sum,
                gout[:], gsel[:].rearrange("p h n -> p n h"), AX_X)]

        def ffn(b, last):
            normed = layer_norm(b)
            xT = transposed(normed, lambda c: xnT[:, 512 * c:512 * c + 512].rearrange("p (n q) -> p n q", q=QB),
                            *last_use["xnT"])
            for t in range(TB):
                mm = pe("gate", [*xT, got_gate, *freed[7]], nc.tensor.matmul,
                    bank[7][:, t * E:(t + 1) * E], xnT[:, t * P:(t + 1) * P], gate[:], start=t == 0,
                    stop=t == TB - 1, skip_group_check=True)
            lg = dve("gate", [mm], nc.vector.tensor_copy,
                logits[:], bank[7][:, 0:TB * E] .rearrange("p (t n) -> p t n", t=TB))
            freed[7] = [lg]
            for t in range(TB):
                tp = dve("top", [lg], nc.vector.max,
                    top[:, t, :], logits[:, t, :])
            for t in range(TB):
                ti = dve("topi", [tp], nc.vector.max_index,
                    topi[:, t, :], top[:, t, :], logits[:, t, :])
            tf = dve("topf", [ti], nc.vector.tensor_copy,
                topf[:], topi[:, :, 0:2])
            wd = dve("wdif", [ti], nc.vector.tensor_tensor,
                wdif[:], top[:, :, 1:2], top[:, :, 0:1], ALU.subtract)
            we = act("wexp", [wd], nc.scalar.activation,
                wexp[:], wdif[:], ACT.Exp)
            ws = dve("wsum", [we], nc.vector.tensor_scalar,
                wsum[:], wexp[:], 1.0, None, ALU.add)
            wa = dve("wtop", [ws], nc.vector.reciprocal,
                wtop[:, 0], wsum[:])
            wb = dve("wtop", [wa], nc.vector.tensor_tensor,
                wtop[:, 1], wexp[:], wtop[:, 0], ALU.mult)
            iota3 = iota_e.rearrange("p (o n) -> p o n", o=1).broadcast_to([P, TB, E])
            for i in range(2):
                ho = dve("hot", [tf], nc.vector.tensor_tensor,
                    hot[:, i], iota3, topf[:, :, i:i + 1].broadcast_to([P, TB, E]), ALU.is_equal)
            for i in range(2):
                hw = dve("hotw", [ho, wb], nc.vector.tensor_tensor,
                    hot[:, i], hot[:, i], wtop[:, i].broadcast_to([P, TB, E]), ALU.mult)
            cwd = dve("cw", [hw], nc.vector.tensor_tensor,
                cw[:], hot[:, 0], hot[:, 1], ALU.add)
            n = 0
            pending = None

            def second(c, ex, r, gelu):
                bk = 4 + r
                for k in range(FC):
                    for i in range(4):
                        mm = pe("w2", [gelu[k], got_w2, *freed[bk]], nc.tensor.matmul,
                            bank[bk][:, i * C:(i + 1) * C], hT[:, r, k, i * P:(i + 1) * P], w2_sb[:, ex, k, :],
                            start=k == 0 and i == 0, stop=k == FC - 1, skip_group_check=True)
                last_use["hT"][r] = [mm]
                for i in range(4):
                    t = 4 * c + i
                    rs = dve("moe", [mm, cwd, moe_prev.get(t)], nc.vector.scalar_tensor_tensor,
                        out=x[:, b * TB + t, :], in0=bank[bk][:, i * C:(i + 1) * C], scalar=cw[:, t, ex:ex + 1],
                        in1=x[:, b * TB + t, :], op0=ALU.mult, op1=ALU.add)
                    moe_prev[t] = rs
                freed[bk] = [rs]
                return rs

            moe_prev = {}
            for c in range(S // 512):
                for ex in range(E):
                    r = n % 2
                    gelu = []
                    for k in range(FC):
                        bk = k
                        mm = pe("w1", [got_w1, *xT, *freed[bk]], nc.tensor.matmul,
                            bank[bk][:], w1_sb[:, ex, k * P:(k + 1) * P], xnT[:, 512 * c:512 * c + 512],
                            start=True, stop=True)
                        ge = act("gelu", [mm, *last_use["hT"][r]], nc.scalar.activation,
                            hT[:, r, k, :], bank[bk][:], ACT.Gelu)
                        freed[bk] = [ge]
                        gelu.append(ge)
                    if pending:
                        second(*pending)
                    pending = (c, ex, r, gelu)
                    n += 1
            rs = second(*pending)
            last_use["xnT"] = [mm]
            x_ready[b] = [rs]
            if last:
                stores.append(dma("store", out_dram[b], x[:, b * TB:(b + 1) * TB, :], rs))

        stores = []
        steps_bias = []
        for m, colset in ((0, qcol), (1, kcol)):
            steps_bias.append(dve("bias", [got_table, zero_cols, got_cols], nc.vector.tensor_scalar,
                gbias[:, 1, m, :], b_cols[:, m, 1:1 + G], colset[0], None, ALU.mult))
        for l in range(2):
            steps_bias.append(dve("bias", [*steps_bias], nc.vector.tensor_scalar,
                gbias[:, l, 1, :], gbias[:, l, 1, :], kcol[2], None, ALU.add))
        bias_set = steps_bias[-1]

        for l in range(2):
            for b in range(B):
                attention(l, b)
                ffn(b, l == 1)
        Q.add("sync", "end", stores, 1, nc.sync.drain)

        block = ctx.enter_context(nc.Block())
        Q.play(nc, ctx, block)


def kernel(**inputs):
    import concourse.bacc as bacc
    from concourse.bass_utils import run_bass_kernel_spmd

    a = {k: np.asarray(v) for k, v in inputs.items()}
    def heads(w):
        return w.reshape(*w.shape[:-1], G, J, D).swapaxes(-3, -2).reshape(w.shape)

    masks, table = constants()
    pa, pb = "L0_attn_a_", "L0_attn_b_"
    plain = np.stack([heads(a[pb + n]) for n in ("bq", "bk")])
    stacks = np.broadcast_to(plain.reshape(2, J, 1, G, D), (2, J, 4, G, D)).transpose(1, 2, 4, 0, 3)
    b_cols = np.concatenate([plain.T.reshape(P, 2, 1), stacks.reshape(P, 2, G)], axis=2)
    arrays = {
        "x_in": a[pa + "x"],
        "w_a": np.stack([heads(a[pa + n].T) for n in ("Wq", "Wk", "Wv")] + [heads(a[pa + "Wo"]).T]),
        "bo_a": a[pa + "bo"].reshape(1, C),
        "w_b": np.stack([heads(a[pb + n]) for n in ("Wq", "Wk", "Wv")] + [heads(a[pb + "Wo"].T).T]),
        "b_b": np.stack([heads(a[pb + n]) for n in ("bq", "bk", "bv")] + [a[pb + "bo"]]),
        "b_cols_in": b_cols,
        "gate_w": a["L0_ffn_gate_w"],
        "w1": a["L0_ffn_w1"],
        "w2": a["L0_ffn_w2"],
        "masks_in": masks,
        "table_in": table,
    }
    nc = bacc.Bacc("TRN2", target_bir_lowering=False, num_devices=1)
    args = []
    for name, arr in arrays.items():
        arrays[name] = np.ascontiguousarray(arr)
        args.append(nc.dram_tensor(name, arr.shape, mybir.dt.from_np(arr.dtype), kind="ExternalInput").ap())
    args.append(nc.dram_tensor("out", (B, S, C), F32, kind="ExternalOutput").ap())
    build(nc, *args)
    return run_bass_kernel_spmd(nc, [arrays], core_ids=[0]).results[0]["out"]
```

```python
from contextlib import ExitStack

import numpy as np

import concourse.bass as bass
from concourse import mybir

F32 = mybir.dt.float32
F32R = mybir.dt.float32r
BF16 = mybir.dt.bfloat16
U32 = mybir.dt.uint32
I32 = mybir.dt.int32
ALU = mybir.AluOpType
ACT = mybir.ActivationFunctionType
AX_X = mybir.AxisListType.X

P = 128
B, S, C = 4, 1024, 128
H, D = 16, 8
J, G = 4, 4
ROWS = P // J
TB = S // P
TT = B * TB
QB = 64
NBLK = S // QB
WIN = 64
PAD = WIN // 2
EXT_A = S + 2 * PAD
KEYS_A = 2 * QB
SPAN_A = P + 2 * PAD
NG = 8
KEYS_B = QB + NG
EXT_B = NBLK * KEYS_B
SPAN_B = 2 * KEYS_B
GLOBALS = [int(v) for v in np.linspace(0, S - 1, NG).astype(np.int64)]
E, F = 8, 512
FC = F // P
U = 2
UT = TT // U
TOP = 2
ST = UT * TOP + E - 1
STEPS = 4
LOT = 3
assert ST % LOT == 0
SCALE = float(D) ** -0.5
EPS = 1e-5
MASKED = -1e30


def constants():
    q, k = np.arange(P)[:, None], np.arange(SPAN_A)[None, :]
    a_max = np.where((k >= q) & (k < q + WIN), 0.0, MASKED)
    q, k = (np.arange(P) % QB)[:, None], np.arange(KEYS_A)[None, :]
    a_exp = np.where((k >= q) & (k < q + WIN), 0.0, MASKED)
    own_keys, own_queries = np.arange(EXT_B) // KEYS_B, np.arange(S) // QB
    patterns = np.zeros((P, EXT_B + S + P))
    for i, pos in enumerate(GLOBALS):
        patterns[0, pos // QB * KEYS_B + QB + i] = MASKED
    patterns[0, EXT_B:EXT_B + S] = 1
    for half in range(2):
        patterns[1 + half, 0:EXT_B] = np.where(own_keys % 2 == half, 0.0, MASKED)
        patterns[1 + half, EXT_B:EXT_B + S] = own_queries % 2 == half
    for i in range(3):
        patterns[i, EXT_B + S + 3 * D + 1 + i::ROWS] = 1
    masks = np.concatenate([a_max, a_exp, np.eye(P), patterns], axis=1)
    chan, row = np.arange(P)[:, None], np.arange(P)[None, :]
    same = (chan // ROWS == row // ROWS) & (chan % D == row % D)
    product = row % ROWS // D
    picks = np.zeros((P, 2, 2, G, P))
    for g in range(G):
        own = same & (chan // D % G == g)
        picks[:, 0, 0, g] = own & ((product == 0) | (product == 2))
        picks[:, 0, 1, g] = own & (product == 1)
        picks[:, 1, 0, g] = own & ((product == 0) | (product == 1))
        picks[:, 1, 1, g] = own & (product == 2)
    cols = np.zeros((P, 2), np.float32)
    cols[:, 1] = np.arange(P) % ROWS == 3 * D
    heads = np.zeros((P, H), np.float32)
    heads[np.arange(P), 4 * ((np.arange(P) // D) % G) + np.arange(P) // ROWS] = 1
    stack = np.zeros((P, G), np.float32)
    stack[np.arange(P), (np.arange(P) // D) % G] = 1
    sums = np.broadcast_to(np.repeat(np.eye(G), D, axis=1).reshape(1, G * ROWS), (P, G * ROWS))
    before = (np.arange(P)[:, None] < np.arange(P)[None, :]).astype(np.float32)
    slot_tiles = np.tile(np.arange(ST, dtype=np.float32), (P, 1))
    experts = np.tile(np.arange(E, dtype=np.float32), (P, 1))
    table = np.concatenate([np.eye(P, dtype=np.float32), cols, heads, stack, experts, sums, before, slot_tiles],
                           axis=1)
    return masks.astype(np.float32), picks.reshape(P, -1).astype(np.float32), np.ascontiguousarray(table.astype(np.float32))


class Token:

    def __init__(self, sem_name, amount):
        self.sem_name, self.amount, self.waited, self.value = sem_name, amount, False, None


class Queues:

    ENGINES = ("sync", "tensor", "vector", "scalar", "gpsimd")

    def __init__(self):
        self.steps = {e: [] for e in self.ENGINES}

    def add(self, engine, stage, after, amount, instruction, *operands, **options):
        token = Token(f"{engine}_{stage}", amount)
        self.steps[engine].append((instruction, operands, options, after, token))
        return token

    def play(self, nc, ctx, block):
        for steps in self.steps.values():
            for _, _, _, after, _ in steps:
                for token in after:
                    if token is not None:
                        token.waited = True
        sems, count = {}, {}
        for engine in self.ENGINES:
            for *_, token in self.steps[engine]:
                if token.waited:
                    name = token.sem_name
                    if name not in sems:
                        sems[name] = ctx.enter_context(nc.semaphore(name))
                    count[name] = count.get(name, 0) + token.amount
                    token.value = count[name]

        def run(engine):
            def body(eng):
                reached = {}
                for instruction, operands, options, after, token in self.steps[engine]:
                    need = {}
                    for t in after:
                        if t is not None:
                            need[t.sem_name] = max(need.get(t.sem_name, 0), t.value)
                    for name, value in need.items():
                        if reached.get(name, 0) < value:
                            eng.wait_ge(sems[name], value)
                            reached[name] = value
                    ins = instruction(*operands, **options)
                    if token.waited:
                        ins.then_inc(sems[token.sem_name], token.amount)
            return body

        block.sync(run("sync"))
        block.tensor(run("tensor"))
        block.vector(run("vector"))
        block.scalar(run("scalar"))
        block.gpsimd(run("gpsimd"))


def build(nc, x_in, w_a, bo_a, w_b, b_b, b_cols_in, gate_w, w1, w2, masks_in, picks_in, table_in, out):
    Q = Queues()

    def pe(stage, after, instruction, *operands, **options):
        return Q.add("tensor", stage, after, 1, instruction, *operands, **options)

    def dve(stage, after, instruction, *operands, **options):
        return Q.add("vector", stage, after, 1, instruction, *operands, **options)

    def act(stage, after, instruction, *operands, **options):
        return Q.add("scalar", stage, after, 1, instruction, *operands, **options)

    def pool(stage, after, instruction, *operands, **options):
        return Q.add("gpsimd", stage, after, 1, instruction, *operands, **options)

    n_dma = [0]

    def dma(name, dst, src, *after):
        n_dma[0] += 1
        return Q.add("sync", f"{name}_{n_dma[0]}", after, 16, nc.sync.dma_start, dst, src)

    with ExitStack() as ctx:
        def sb(name, shape, dt=F32):
            return ctx.enter_context(nc.sbuf_tensor(name, shape, dt))

        x = sb("x", [P, TT, C])
        xn = sb("xn", [P, TB, C])
        ext = sb("ext", [P, EXT_B])
        kst = sb("kst", [P, G, EXT_B], F32R)
        qst = sb("qst", [P, G, S], F32R)
        qsl = sb("qsl", [P, 2, G, J, P], F32R)
        hi = sb("hi", [P, 2, 512], F32R)
        lo = sb("lo", [P, 2, 512], F32R)
        picks = sb("picks", [P, 2, 2, G, P], F32R)
        v = sb("v", [P, NBLK, C])
        pt = sb("pt", [P, 2, G, J * P])
        rden = sb("rden", [P, 2, P])
        on = sb("on", [P, 2, P])
        mx = sb("mx", [P, J, G, TB])
        mxT = sb("mxT", [P, P], F32R)
        w_attn = [sb(f"w_attn{l}", [P, 4, C]) for l in range(2)]
        b_nat = sb("b_nat", [P, 3, C])
        b_cols = sb("b_cols", [P, 2])
        gate = sb("gate", [P, E])
        w1_sb = sb("w1_sb", [P, E, F])
        w2_sb = sb("w2_sb", [P, E, FC, C])
        masks = sb("masks", [P, SPAN_A + KEYS_A + P], BF16)
        patterns = sb("patterns", [3, EXT_B + S + P], BF16)
        table = sb("table", [P, P + 2 + H + G + E + G * ROWS + P + ST])
        power = sb("power", [P, TB])
        stats = sb("stats", [P, TB, 6])
        mv = sb("mv", [P, TB, 2])
        veps = sb("veps", [P, TB])
        rstd = sb("rstd", [P, TB])
        gq = sb("gq", [P, NG])
        gbd = sb("gbd", [P, H, NG])
        gp = sb("gp", [P, S])
        gs = sb("gs", [P, 4])
        gpT = sb("gpT", [QB, NBLK, P])
        gsel = sb("gsel", [P, H, NG])
        gout = sb("gout", [P, NG])
        fxn = sb("fxn", [P, UT, C])
        gT = sb("gT", [P, 2, 512])
        logits = sb("logits", [P, UT, E])
        top = sb("top", [P, UT, 8])
        topi = sb("topi", [P, UT, 8], U32)
        topf = sb("topf", [P, UT, TOP])
        wdif = sb("wdif", [P, UT, 1])
        wexp = sb("wexp", [P, UT, 1])
        wsum = sb("wsum", [P, UT, 1])
        wtop = sb("wtop", [P, U, TOP, UT, 1])
        hot = sb("hot", [P, TOP, UT, E])
        both = sb("both", [P, UT, E])
        whole = sb("whole", [P, UT, E])
        upto = sb("upto", [P, UT, E])
        rank = sb("rank", [P, UT, E])
        ones = sb("ones", [P, P])
        n_int = sb("n_int", [P, 2, E], U32)
        n_flt = sb("n_flt", [P, 3, E])
        hit = sb("hit", [P, UT, E])
        slot_f = sb("slot_f", [P, TOP, UT])
        slot = sb("slot", [P, U, TOP, UT], U32)
        passed = sb("passed", [1, ST, E])
        owner_f = sb("owner_f", [1, 2, ST])
        owner = sb("owner", [1, U, ST], I32)
        shared, at = pt[:].rearrange("p r g n -> p (r g n)"), 0
        tile_views = []
        for n in (LOT * C, P, F, F, F):
            tile_views.append(shared[:, at:at + 2 * n].rearrange("p (r n) -> p r n", r=2))
            at += 2 * n
        xs, xsT, w1_own, w2_own, hidT = tile_views
        xs = xs.rearrange("p r (n c) -> p r n c", c=C)
        ys = sb("ys", [P, 2, LOT, C])
        got = sb("got", [P, 4, TOP, C])

        xs_dram = [nc.dram_tensor(f"xs_dram{u}", (ST * P, C), F32, kind="Internal").ap() for u in range(U)]
        ys_dram = [nc.dram_tensor(f"ys_dram{u}", (ST * P, C), F32, kind="Internal").ap() for u in range(U)]

        bank = [ctx.enter_context(nc.psum_tensor(f"bank{i}", [P, 512], F32)) for i in range(8)]
        freed = [[] for _ in range(8)]

        a_max, a_exp = masks[:, 0:SPAN_A], masks[:, SPAN_A:SPAN_A + KEYS_A]
        eye16 = masks[:, SPAN_A + KEYS_A:]
        pattern_of = patterns[:, EXT_B:EXT_B + S], patterns[:, 0:EXT_B]
        into_rows = patterns[:, EXT_B + S:]
        eye = table[:, 0:P]
        no_bias, one_row = table[:, P:P + 1], table[:, P + 1:P + 2]
        at = P + 2
        table_ap = []
        for n in (H, G, E, G * ROWS, P, ST):
            table_ap.append(table[:, at:at + n])
            at += n
        head_of, stack_of, iota_e, stack_sums, before, iota_s = table_ap
        stack_sums = stack_sums.rearrange("p (g c) -> p g c", g=G)

        x_dram = x_in.rearrange("b (t p) c -> b p t c", p=P)
        out_dram = out.rearrange("b (t p) c -> b p t c", p=P)
        got_x = [dma("x", x[:, b * TB:(b + 1) * TB, :], x_dram[b]) for b in range(1)]
        got_table = dma("table", table[:], table_in)
        got_w = [dma("wa", w_attn[0][:], w_a.rearrange("m c e -> c m e"))]
        staged = pt[:, 0].rearrange("p j n -> p (j n)")
        n_mask, n_pattern = masks.shape[1], patterns.shape[1]
        masks_landed = dma("masks", staged[:, 0:n_mask], masks_in[:, 0:n_mask])
        staged_picks = pt[:, 1].rearrange("p j n -> p (j n)")
        picks_landed = dma("picks", staged_picks, picks_in)
        staged_patterns = [(fxn[0:3].rearrange("p t c -> p (t c)")[:, 0:EXT_B], slice(0, EXT_B)),
                           (v[0:3].rearrange("p n c -> p (n c)")[:, 0:S + P], slice(EXT_B, n_pattern))]
        patterns_landed = [dma("patterns", to, masks_in[0:3, n_mask + part.start:n_mask + part.stop])
                           for to, part in staged_patterns]
        got_x += [dma("x", x[:, b * TB:(b + 1) * TB, :], x_dram[b]) for b in range(1, B)]
        got_bo = [dma("bo", b_nat[:, 0, :], bo_a.broadcast_to([P, C]))]
        got_gate = dma("gate", gate[:], gate_w)
        got_w1 = dma("w1", w1_sb[:], w1.rearrange("e c f -> c e f"))
        got_w2 = dma("w2", w2_sb[:], w2.rearrange("e (k f) c -> f e k c", f=P))
        got_w.append(dma("wb", w_attn[1][:], w_b.rearrange("m c e -> c m e")))
        got_bo.append(dma("bo", b_nat[:, 1, :], b_b[3:4, :].broadcast_to([P, C])))
        got_bias = dma("bv", b_nat[:, 2, :], b_b[2:3, :].broadcast_to([P, C]))
        got_cols = dma("bcols", b_cols[:], b_cols_in)

        ones_set = dve("ones", [], nc.vector.memset,
            ones[:], 1.0)
        blank = dve("blank", [], nc.vector.memset, qsl[:].rearrange("p r g j q -> p (r g j q)").bitcast(F32), 0.0)
        zeros = qsl[:].rearrange("p r g j q -> p (r g j q)").bitcast(F32)
        n_zeros = zeros.shape[1]
        slots_of = [xs_dram[u].rearrange("(p n) c -> p (n c)", p=P) for u in range(U)]
        zeroed = [[Q.add("sync", f"zeroed{u}", [blank], 16, nc.sync.dma_start,
                         slots_of[u][:, at:min(at + n_zeros, ST * C)], zeros[:, 0:min(n_zeros, ST * C - at)])
                   for at in range(0, ST * C, n_zeros)] for u in range(U)]
        power_set = dve("power", [], nc.vector.memset,
            power[:], -0.5)
        got_masks = dve("masks", [masks_landed], nc.vector.tensor_copy, masks[:], staged[:, 0:n_mask])
        for landed, (staged_part, part) in zip(patterns_landed, staged_patterns):
            got_patterns = dve("patterns", [landed], nc.vector.tensor_copy, patterns[:, part], staged_part)
        got_picks = act("picks", [picks_landed], nc.scalar.copy,
            picks[:].rearrange("p m h g n -> p (m h g n)"), staged_picks)
        x_ready = [[got_x[b]] for b in range(B)]

        def moments(b):
            for t in range(TB):
                st = dve("bn", [*x_ready[b]], nc.vector.bn_stats, stats[:, t, :], x[:, b * TB + t, :])
            for t in range(TB):
                ag = dve("agg", [st], nc.vector.bn_aggr, mv[:, t, :], stats[:, t, :])
            ve = dve("veps", [ag, *rstd_read], nc.vector.tensor_scalar, veps[:], mv[:, :, 1], EPS, None, ALU.add)
            rstd_set[:] = [pool("rstd", [ve, power_set], nc.gpsimd.tensor_tensor,
                                rstd[:], veps[:], power[:], ALU.pow)]

        def norm(b, to, to_free):
            done = [dve("norm", [*rstd_set, *to_free], nc.vector.tensor_scalar,
                        to[:, t, :], x[:, b * TB + t, :], mv[:, t, 0:1], rstd[:, t:t + 1], ALU.subtract, ALU.mult)
                    for t in range(TB)]
            rstd_read[:] = [done[-1]]
            return done

        rstd_set, rstd_read, xn_read = [], [], []

        def turn_tokens(chunk, normed, banks, dst, dst_free):
            bk = banks[chunk % 2]
            for t in range(4 * chunk, 4 * chunk + 4):
                tr = pe("xT", [normed[t], got_table, *freed[bk]], nc.tensor.transpose,
                        bank[bk][:, (t % 4) * P:(t % 4 + 1) * P], xn[:, t, :], eye)
            freed[bk] = [act("xT", [tr, *dst_free], nc.scalar.copy,
                             dst, bank[bk][:].rearrange("p (n q) -> p n q", q=QB))]
            xn_read[:] = [tr]
            return freed[bk][0]

        last_use = {"ext": [], "kst": [], "qst": [], "v": [got_patterns], "on": [[], []], "mxT": [], "xnT": [], "qsl": [zeroed[0] + zeroed[1]] * 2, "pt": [[got_masks], [got_picks]],
                    "rden": [[], []], "hT": [[], []], "hi": [[], []],
                    "fxn": [got_patterns], "gT": [[], []], "w1_own": [[], []], "w2_own": [[], []], "wexp": [], "slot": [[], []], "owner": [[], []], "xs": [[], []],
                    "xsT": [[], []], "hidT": [[], []], "ys": [[], []], "got": [[], [], [], []]}

        def ext_body(l, c):
            if l == 0:
                return ext[:, PAD + 512 * c:PAD + 512 * c + 512].rearrange("p (n q) -> p n q", q=QB)
            return ext[:, 0:EXT_B].rearrange("p (n k) -> p n k", k=KEYS_B)[:, 8 * c:8 * c + 8, 0:QB]

        def prepare(l, b):
            normed, copies = [], []

            def turn(chunk):
                return lambda banks: copies.append(
                    turn_tokens(chunk, normed, banks, ext_body(l, chunk), last_use["ext"]))

            def edges(banks):
                ext_full = list(copies)
                if l == 0:
                    ext_full.append(dve("edge", [copies[0]], nc.vector.tensor_copy,
                                        ext[:, 0:PAD], ext[:, PAD:PAD + 1].broadcast_to([P, PAD])))
                    ext_full.append(dve("edge", [copies[1]], nc.vector.tensor_copy, ext[:, PAD + S:EXT_A],
                                        ext[:, PAD + S - 1:PAD + S].broadcast_to([P, PAD])))
                else:
                    blocks = ext[:, 0:EXT_B].rearrange("p (n k) -> p n k", k=KEYS_B)
                    for i, pos in enumerate(GLOBALS):
                        src = (pos // QB) * KEYS_B + pos % QB
                        ext_full.append(dve("edge", [copies[pos // 512]], nc.vector.tensor_copy,
                                            blocks[:, :, QB + i], ext[:, src:src + 1].broadcast_to([P, NBLK])))
                prepared[l, b] = normed, ext_full

            return [lambda banks: moments(b), lambda banks: normed.extend(norm(b, xn, xn_read)),
                    *(turn(c) for c in range(TB // 4)), edges]

        def attention(l, b):
            keys, ext_n, span = ((KEYS_A, EXT_A, SPAN_A), (KEYS_B, EXT_B, SPAN_B))[l]
            step = (QB, KEYS_B)[l]
            normed, ext_full = prepared[l, b]
            chunks = [(0, 512 * c, 512, ext_body(l, c) if l else ext[:, PAD + 512 * c:PAD + 512 * c + 512])
                      for c in range(S // 512)]
            chunks += [(1, at, min(512, ext_n - at), ext[:, at:min(at + 512, ext_n)]) for at in range(0, ext_n, 512)]

            def plain(i):
                m, at, n, view = chunks[i]
                bk, r = 4 + i % 2, i % 2
                bias = b_cols[:, m:m + 1] if l else no_bias
                mm = pe("proj", [got_w[l], *ext_full, *freed[bk]], nc.tensor.matmul,
                        bank[bk][:, 0:n], w_attn[l][:, m, :], view, start=True, stop=True)
                hd = act("hi", [mm, got_cols, got_table, *last_use["hi"][r]], nc.scalar.activation,
                         hi[:, r, 0:n], bank[bk][:, 0:n], ACT.Identity, bias=bias)
                ld = dve("lo", [hd], nc.vector.scalar_tensor_tensor,
                         out=lo[:, r, 0:n], in0=bank[bk][:, 0:n], scalar=bias, in1=hi[:, r, 0:n].bitcast(F32),
                         op0=ALU.add, op1=ALU.subtract)
                freed[bk] = [ld]
                return ld

            def spread(i, split):
                m, at, n, _ = chunks[i]
                r, dst = i % 2, (qst, kst)[m]
                done = []
                for g in range(G):
                    pe("spread", [split, got_picks, *freed[g]], nc.tensor.matmul,
                       bank[g][:, 0:n], picks[:, m, 0, g, :], hi[:, r, 0:n], start=True, stop=False)
                    mm = pe("spread", [], nc.tensor.matmul,
                            bank[g][:, 0:n], picks[:, m, 1, g, :], lo[:, r, 0:n], start=False, stop=l == 0)
                    if l == 1:
                        mm = pe("spread", [got_patterns], nc.tensor.matmul, bank[g][:, 0:n], into_rows,
                                pattern_of[m][:, at:at + n], start=False, stop=True)
                    free = last_use[("qst", "kst")[m]]
                    if g % 2:
                        cp = act("spread", [mm, *free], nc.scalar.activation,
                                 dst[:, g, at:at + n], bank[g][:, 0:n], ACT.Identity,
                                 bias=one_row if m else no_bias)
                    else:
                        cp = dve("spread", [mm, *free], nc.vector.tensor_scalar,
                                 dst[:, g, at:at + n], bank[g][:, 0:n], one_row if m else no_bias, None, ALU.add)
                    freed[g] = [cp]
                    done.append(cp)
                last_use["hi"][r] = [mm]
                return done[-2:]

            split, stacks_set = plain(0), [None, None]
            for i in range(len(chunks)):
                ahead = plain(i + 1) if i + 1 < len(chunks) else None
                stacks_set[chunks[i][0]] = spread(i, split)
                split = ahead
            q_set, k_set = stacks_set
            for c in range(NBLK // 4):
                bk = 6 + c % 2
                for i in range(4):
                    blk = 4 * c + i
                    mm = pe("v", [got_w[l], *ext_full, *freed[bk]], nc.tensor.matmul,
                        bank[bk][0:keys, i * C:(i + 1) * C], ext[:, blk * step:blk * step + keys],
                        w_attn[l][:, 2, :], start=i == 0, stop=i == 3, skip_group_check=True)
                src = bank[bk][0:keys, :].rearrange("p (n c) -> p n c", c=C)
                if l == 0:
                    v_set = act("v", [mm, *last_use["v"]], nc.scalar.copy,
                        v[0:keys, 4 * c:4 * c + 4, :], src)
                else:
                    v_set = dve("v", [mm, got_bias, *last_use["v"]], nc.vector.tensor_tensor,
                        v[0:keys, 4 * c:4 * c + 4, :], src, b_nat[0:keys, 2:3, :].broadcast_to([keys, 4, C]),
                        ALU.add)
                freed[bk] = [v_set]
            last_use["ext"] = [mm]
            g_done = global_queries(b, ext_full, v_set) if l else []

            for t in range(TB):
                for _ in range(UT // TB):
                    if background:
                        background.pop(0)(None)
                for gp2 in range(G // 2):
                    for j in range(J if l == 0 else 0):
                        bk = j + 4 * gp2
                        pe("mmask", [got_masks, *freed[bk]], nc.tensor.matmul,
                           bank[bk][:, 0:2 * span], eye16,
                           a_max.rearrange("p (o k) -> p o k", o=1).broadcast_to([P, 2, span]), start=True,
                           stop=False, skip_group_check=True)
                    for i in range(2):
                        g = 2 * gp2 + i
                        first = t * P if l == 0 else 2 * t * KEYS_B
                        for j in range(J):
                            bk, r = j + 4 * gp2, slice(j * ROWS, (j + 1) * ROWS)
                            mm = pe("mscore", [*q_set, *k_set, *freed[bk]], nc.tensor.matmul,
                                bank[bk][:, i * span:(i + 1) * span], qst[r, g, t * P:(t + 1) * P],
                                kst[r, g, first:first + span], start=l == 1 and i == 0, stop=i == 1, skip_group_check=True,
                                tile_position=(r.start, 0))
                            if i == 1:
                                md = dve("max", [mm], nc.vector.reduce_max,
                                    mx[:, j, 2 * gp2:2 * gp2 + 2, t],
                                    bank[bk][:, 0:2 * span].rearrange("p (g k) -> p g k", g=2), AX_X)
                                freed[bk] = [md]
            tr = pe("mT", [md, *freed[7]], nc.tensor.transpose,
                bank[7][:, 0:P], mx[:].rearrange("p j g t -> p (j g t)"), eye)
            neg = dve("neg", [tr, *last_use["mxT"]], nc.vector.tensor_scalar,
                mxT[:], bank[7][:, 0:P], -1.0, None, ALU.mult)
            freed[7] = [neg]
            rows = [Q.add("sync", "mrow", [neg, mm], 16, nc.sync.dma_start, qst[j * ROWS + 3 * D:j * ROWS + 3 * D + 1, :, :].rearrange("o g s -> o (g s)")
                        .rearrange("o (r q) -> o r q", q=P).bitcast(F32), mxT[32 * j:32 * j + 32, :].bitcast(F32))
                    for j in range(J)]
            last_use["mxT"] = rows

            biased = pool("bo", [*normed, got_bo[l]], nc.gpsimd.tensor_tensor,
                          x[:, b * TB:(b + 1) * TB, :], x[:, b * TB:(b + 1) * TB, :],
                          b_nat[:, l:l + 1, :].broadcast_to([P, TB, C]), ALU.add)

            slotted = {}

            def slots(t):
                for j in range(J):
                    r = slice(j * ROWS, (j + 1) * ROWS)
                    slotted[t] = dve("slots", [*rows, *last_use["qsl"][t % 2]], nc.vector.tensor_copy,
                                     qsl[r, t % 2, :, j, :], qst[r, :, t * P:(t + 1) * P])

            def numerators(t):
                r2 = t % 2
                for g in range(G if l == 0 else 0):
                    pe("emask", [*freed[g]], nc.tensor.matmul,
                       bank[g][:], a_exp, eye16.rearrange("p (o q) -> p o q", o=1).broadcast_to([P, J, P]),
                       start=True, stop=False, skip_group_check=True)
                exps = []
                for g in range(G):
                    for h in range(2):
                        blk = 2 * t + h
                        mm = pe("escore", [slotted[t], *freed[g]], nc.tensor.matmul,
                                bank[g][0:keys, :].rearrange("p (j b q) -> p j b q", j=J, b=2)[:, :, h, :],
                                kst[:, g, blk * step:blk * step + keys], qsl[:, r2, g, :, h * QB:(h + 1) * QB],
                                start=l == 1 and h == 0, stop=h == 1, skip_group_check=True)
                    exps.append(act("exp", [mm, *last_use["pt"][r2]], nc.scalar.activation,
                                    pt[0:keys, r2, g, :], bank[g][0:keys, :], ACT.Exp, scale=SCALE))
                    freed[g] = [exps[g]]
                last_use["qsl"][r2] = [mm]
                return exps

            def values(t, exps):
                r2 = t % 2
                nb, db = 4 + 2 * r2, 5 + 2 * r2
                num, den = bank[nb], bank[db]
                for j in range(J):
                    c = slice(j * ROWS, (j + 1) * ROWS)
                    for g in range(G):
                        mm = pe("den", [exps[g], got_table, *freed[db]], nc.tensor.matmul,
                                den[c, 0:P], stack_sums[0:keys, g, :], pt[0:keys, r2, g, j * P:(j + 1) * P],
                                start=g == 0, stop=g == G - 1, skip_group_check=True, tile_position=(0, c.start))
                rc = dve("rden", [mm], nc.vector.reciprocal, rden[:, r2, :], den[:, 0:P])
                freed[db] = [rc]
                for h in range(2):
                    for j in range(J):
                        c = slice(j * ROWS, (j + 1) * ROWS)
                        pcol = pt[0:keys, r2, :, j * P + h * QB:j * P + (h + 1) * QB]
                        ncol = num[c, :].rearrange("p (g b q) -> p g b q", g=G, b=2)[:, :, h, :]
                        mm = pe("pv", [v_set, *freed[nb]], nc.tensor.matmul,
                                ncol, v[0:keys, 2 * t + h, c], pcol, start=h == 0, stop=h == 1,
                                skip_group_check=True, tile_position=(0, c.start))
                last_use["pt"][r2] = [mm]
                on_set = None
                for g in range(G):
                    stack = num[:, g * P:(g + 1) * P], stack_of[:, g:g + 1]
                    if g == 0:
                        on_set = dve("own", [mm, *last_use["on"][r2]], nc.vector.tensor_scalar,
                                     on[:, r2, :], *stack, None, ALU.mult)
                    else:
                        on_set = dve("own", [on_set], nc.vector.scalar_tensor_tensor, on[:, r2, :], *stack,
                                     on[:, r2, :], ALU.mult, ALU.add)
                freed[nb] = [on_set]
                on_set = dve("on", [on_set, rc], nc.vector.tensor_tensor,
                             on[:, r2, :], on[:, r2, :], rden[:, r2, :], ALU.mult)
                for i, pos in enumerate(GLOBALS if l else []):
                    if pos // P == t:
                        on_set = dve("gput", [on_set, *g_done], nc.vector.tensor_copy,
                                     on[:, r2, pos % P:pos % P + 1], gout[:, i:i + 1])
                return mm, on_set

            def output(t, on_set):
                r2 = t % 2
                nb = 4 + 2 * r2
                wo = pe("wo", [on_set, got_w[l]], nc.tensor.matmul,
                        bank[nb][:, 0:C], on[:, r2, :], w_attn[l][:, 3, :], start=True, stop=True)
                last_use["on"][r2] = [wo]
                rs = dve("resid", [wo, biased], nc.vector.tensor_tensor,
                         x[:, b * TB + t, :], x[:, b * TB + t, :], bank[nb][:, 0:C], ALU.add)
                freed[nb] = [rs]
                return rs

            slots(0)
            slots(1)
            exps, on_set = numerators(0), None
            for t in range(TB):
                ahead = numerators(t + 1) if t + 1 < TB else None
                if t + 2 < TB:
                    slots(t + 2)
                mm, on_next = values(t, exps)
                if on_set:
                    output(t - 1, on_set)
                exps, on_set = ahead, on_next
                other = 6 - 2 * (t % 2)
                for _ in range(min(len(alongside), STEPS)):
                    alongside.pop(0)((other, other + 1))
            rs = output(TB - 1, on_set)
            last_use["kst"] = last_use["qst"] = last_use["v"] = [mm]
            x_ready[b] = [rs]

        def global_queries(b, ext_full, v_set):
            for c in range(S // 512):
                bk = 4 + c % 2
                src = ext[:, 0:EXT_B].rearrange("p (n k) -> p n k", k=KEYS_B)[:, 8 * c:8 * c + 8, 0:QB]
                mm = pe("gk", [*freed[bk]], nc.tensor.matmul,
                    bank[bk][:], w_attn[1][:, 1, :], src, start=True, stop=True)
                kp = act("gk", [mm, got_cols], nc.scalar.activation,
                    gp[:, 512 * c:512 * c + 512], bank[bk][:], ACT.Identity, bias=b_cols[:, 1:2])
                freed[bk] = [kp]
            mm = pe("gq", [*freed[6]], nc.tensor.matmul,
                bank[6][:, 0:NG], w_attn[1][:, 0, :], ext[:, QB:KEYS_B], start=True, stop=True)
            gqd = dve("gq", [mm, got_cols], nc.vector.tensor_scalar,
                gq[:], bank[6][:, 0:NG], b_cols[:, 0:1], None, ALU.add)
            freed[6] = [gqd]
            bd = dve("gbd", [gqd], nc.vector.tensor_tensor,
                gbd[:], gq[:].rearrange("p (o n) -> p o n", o=1).broadcast_to([P, H, NG]),
                head_of.rearrange("p (h o) -> p h o", o=1).broadcast_to([P, H, NG]), ALU.mult)
            gbd2 = gbd[:].rearrange("p h n -> p (h n)")
            for c in range(2):
                mm = pe("gs", [bd, kp, *freed[c]], nc.tensor.matmul,
                    bank[c][:], gbd2, gp[:, 512 * c:512 * c + 512], start=True, stop=True)
                g1 = dve("gmax", [mm], nc.vector.reduce_max,
                    gs[:, c:c + 1], bank[c][:], AX_X)
            g2 = dve("gmax", [g1], nc.vector.tensor_tensor,
                gs[:, 2:3], gs[:, 0:1], gs[:, 1:2], ALU.max)
            g3 = dve("gmax", [g2], nc.vector.tensor_scalar,
                gs[:, 3:4], gs[:, 2:3], -SCALE, None, ALU.mult)
            for c in range(2):
                ex = act("gexp", [g3], nc.scalar.activation,
                    gp[:, 512 * c:512 * c + 512], bank[c][:], ACT.Exp, bias=gs[:, 3:4], scale=SCALE)
                freed[c] = [ex]
            g4 = dve("gsum", [ex], nc.vector.reduce_sum,
                gs[:, 0:1], gp[:], AX_X)
            g5 = dve("gsum", [g4], nc.vector.reciprocal,
                gs[:, 1:2], gs[:, 0:1])
            g6 = dve("gnorm", [g5], nc.vector.tensor_scalar,
                gp[:], gp[:], gs[:, 1:2], None, ALU.mult)
            for c in range(4):
                for i in range(4):
                    n = 4 * c + i
                    tr = pe("gT", [g6, *freed[c]], nc.tensor.transpose,
                        bank[c][0:QB, i * P:(i + 1) * P], gp[:, n * QB:(n + 1) * QB], eye)
                cp = act("gT", [tr], nc.scalar.copy,
                    gpT[:, 4 * c:4 * c + 4, :], bank[c][0:QB, :] .rearrange("p (n q) -> p n q", q=P))
                freed[c] = [cp]
            for n in range(NBLK):
                mm = pe("gpv", [cp, v_set, *freed[6]], nc.tensor.matmul,
                    bank[6][:, 0:P], v[0:QB, n, :], gpT[:, n, :], start=n == 0, stop=n == NBLK - 1)
            sl = dve("gsel", [mm], nc.vector.tensor_tensor,
                gsel[:], bank[6][:, 0:P].rearrange("p (h n) -> p h n", h=H),
                head_of.rearrange("p (h o) -> p h o", o=1).broadcast_to([P, H, NG]), ALU.mult)
            freed[6] = [sl]
            return [dve("gout", [sl], nc.vector.reduce_sum,
                gout[:], gsel[:].rearrange("p h n -> p n h"), AX_X)]

        def route(l, u):
            normed, seen = [], {}

            def norm_to_fxn(n):
                b = u * B // U + n
                return [lambda banks: moments(b),
                        lambda banks: normed.extend(norm(b, fxn[:, n * TB:(n + 1) * TB, :], last_use["fxn"]))]

            def turn(c):
                def do(banks):
                    bk, r = banks[0], c % 2
                    for t in range(4 * c, 4 * c + 4):
                        tr = pe("gT", [normed[t], *freed[bk]], nc.tensor.transpose,
                                bank[bk][:, (t % 4) * P:(t % 4 + 1) * P], fxn[:, t, :], eye)
                    seen["turned", c] = act("gT", [tr, *last_use["gT"][r]], nc.scalar.copy, gT[:, r, :], bank[bk][:])
                    freed[bk] = [seen["turned", c]]
                return do

            def gates(c):
                def do(banks):
                    bk, r = banks[1], c % 2
                    for t in range(4):
                        mm = pe("gate", [seen["turned", c], got_gate, *freed[bk]], nc.tensor.matmul,
                                bank[bk][:, t * E:(t + 1) * E], gT[:, r, t * P:(t + 1) * P], gate[:],
                                start=t == 0, stop=t == 3, skip_group_check=True)
                    last_use["gT"][r] = [mm]
                    lg = dve("gate", [mm], nc.vector.tensor_copy, logits[:, 4 * c:4 * c + 4, :],
                             bank[bk][:, 0:4 * E].rearrange("p (t n) -> p t n", t=4))
                    freed[bk] = [lg]
                    for t in range(4 * c, 4 * c + 4):
                        tp = dve("top", [lg], nc.vector.max, top[:, t, :], logits[:, t, :])
                    for t in range(4 * c, 4 * c + 4):
                        seen["top"] = dve("topi", [tp], nc.vector.max_index,
                                          topi[:, t, :], top[:, t, :], logits[:, t, :])
                return do

            def weigh(banks):
                ti = seen["top"]
                tf = dve("topf", [ti], nc.vector.tensor_copy, topf[:], topi[:, :, 0:TOP])
                wd = dve("wdif", [ti, *last_use["wexp"]], nc.vector.tensor_tensor,
                         wdif[:], top[:, :, 1:2], top[:, :, 0:1], ALU.subtract)
                we = act("wexp", [wd], nc.scalar.activation, wexp[:], wdif[:], ACT.Exp)
                iota3 = iota_e.rearrange("p (o n) -> p o n", o=1).broadcast_to([P, UT, E])
                for i in range(TOP):
                    ho = dve("hot", [tf, got_table], nc.vector.tensor_tensor,
                             hot[:, i], iota3, topf[:, :, i:i + 1].broadcast_to([P, UT, E]), ALU.is_equal)
                seen["both"] = dve("both", [ho], nc.vector.tensor_tensor, both[:], hot[:, 0], hot[:, 1], ALU.add)
                ws = dve("wsum", [we], nc.vector.tensor_scalar, wsum[:], wexp[:], 1.0, None, ALU.add)
                wa = dve("wtop", [ws], nc.vector.reciprocal, wtop[:, u, 0], wsum[:])
                wb = dve("wtop", [wa], nc.vector.tensor_tensor, wtop[:, u, 1], wexp[:], wtop[:, u, 0], ALU.mult)
                last_use["wexp"] = [wb]

            def count(banks):
                b0, b1 = banks
                flat = both[:].rearrange("p t n -> p (t n)")
                pe("rank", [seen["both"], *freed[b0]], nc.tensor.matmul,
                   bank[b0][:, 0:UT * E], before, flat, start=True, stop=True)
                mm = pe("rank", [ones_set, *freed[b1]], nc.tensor.matmul,
                        bank[b1][:, 0:UT * E], ones[:], flat, start=True, stop=True)
                wh = dve("whole", [mm], nc.vector.tensor_copy,
                         whole[:].rearrange("p t n -> p (t n)"), bank[b1][:, 0:UT * E])
                freed[b1] = [wh]
                rk = dve("rank", [mm], nc.vector.tensor_copy,
                         rank[:].rearrange("p t n -> p (t n)"), bank[b0][:, 0:UT * E])
                freed[b0] = [rk]
                for n in range(E):
                    seen["upto"] = dve("upto", [wh], nc.vector.tensor_tensor_scan,
                                       upto[:, :, n], ones[:, 0:UT], whole[:, :, n], 0.0, ALU.mult, ALU.add)
                last_use["fxn"] = [mm]

            def place(banks):
                up = seen["upto"]
                r1 = dve("rank", [up], nc.vector.tensor_tensor, rank[:], rank[:], upto[:], ALU.add)
                r2 = dve("rank", [r1], nc.vector.tensor_tensor, rank[:], rank[:], whole[:], ALU.subtract)
                n1 = dve("tiles", [up], nc.vector.tensor_scalar,
                         n_int[:, 0], upto[:, UT - 1, :], P - 1.0, None, ALU.add)
                n2 = dve("tiles", [n1], nc.vector.tensor_scalar,
                         n_int[:, 1], n_int[:, 0], P.bit_length() - 1, None, ALU.logical_shift_right)
                n3 = dve("tiles", [n2], nc.vector.tensor_copy, n_flt[:, 0], n_int[:, 1])
                n4 = dve("tiles", [n3], nc.vector.tensor_tensor_scan,
                         n_flt[:, 1], ones[:, 0:E], n_flt[:, 0], 0.0, ALU.mult, ALU.add)
                n5 = dve("tiles", [n4], nc.vector.tensor_tensor, n_flt[:, 2], n_flt[:, 1], n_flt[:, 0], ALU.subtract)
                r3 = dve("rank", [r2, n5], nc.vector.scalar_tensor_tensor,
                         out=rank[:], in0=n_flt[:, 2:3, :].broadcast_to([P, UT, E]), scalar=float(P), in1=rank[:],
                         op0=ALU.mult, op1=ALU.add)
                sl = None
                for i in range(TOP):
                    own = dve("slot", [r3, sl], nc.vector.tensor_tensor, hit[:], hot[:, i], rank[:], ALU.mult)
                    sl = dve("slot", [own], nc.vector.reduce_sum, slot_f[:, i, :], hit[:], AX_X)
                placed = dve("placed", [sl, *last_use["slot"][u]], nc.vector.tensor_copy, slot[:, u], slot_f[:])
                o1 = dve("owner", [n4], nc.vector.tensor_tensor,
                         passed[:], iota_s[0:1, :].rearrange("p (s o) -> p s o", o=1).broadcast_to([1, ST, E]),
                         n_flt[0:1, 1:2, :].broadcast_to([1, ST, E]), ALU.is_ge)
                o2 = dve("owner", [o1], nc.vector.reduce_sum, owner_f[:, 0, :], passed[:], AX_X)
                o3 = dve("owner", [o2], nc.vector.tensor_scalar,
                         owner_f[:, 1, :], owner_f[:, 0, :], E - 1.0, float(F), ALU.min, ALU.mult)
                owned = dve("owner", [o3, *last_use["owner"][u]], nc.vector.tensor_copy, owner[:, u, :], owner_f[:, 1, :])
                routed[u] = (normed, placed, owned)

            steps = [step for n in range(B // U) for step in norm_to_fxn(n)]
            steps.append(turn(0))
            for c in range(1, UT // 4):
                steps += [turn(c), gates(c - 1)]
            return [*steps, gates(UT // 4 - 1), weigh, count, place]

        def scatter(l, u):
            normed, placed, _ = routed[u]
            scattered[u] = []
            for t in range(UT):
                for i in range(TOP):
                    scattered[u].append(Q.add(
                        "gpsimd", f"scatter{l}{u}", [normed[-1], placed, *zeroed[u], *xs_read[u]], 16,
                        nc.gpsimd.indirect_dma_start, xs_dram[u],
                        bass.IndirectOffsetOnAxis(slot[:, u, i, t:t + 1], 0), fxn[:, t, :], None))
            last_use["fxn"] = scattered[u]

        def experts(l, u):
            owned = routed[u][2]
            xs_tiles = xs_dram[u].rearrange("(n p) c -> p n c", p=P)
            ys_tiles = ys_dram[u].rearrange("(n p) c -> p n c", p=P)
            w1_flat = w1_sb[:].rearrange("c e f -> c (e f)")
            w2_flat = w2_sb[:].rearrange("f e k c -> f (e k c)")
            loaded, turned, hidden, weights = {}, {}, {}, {}

            def load(n):
                loaded[n] = Q.add("sync", f"xs{n % 2}", [*scattered[u], *last_use["xs"][n % 2]], 16,
                                  nc.sync.dma_start, xs[:, n % 2, :, :], xs_tiles[:, n * LOT:(n + 1) * LOT, :])

            def turn(n):
                if n % LOT == 0 and n // LOT + 1 < ST // LOT:
                    load(n // LOT + 1)
                lot, r = n // LOT, n % 2
                tr = pe("xsT", [loaded[lot], *freed[r]], nc.tensor.transpose,
                        bank[r][:, 0:P], xs[:, lot % 2, n % LOT, :], eye)
                last_use["xs"][lot % 2] = [tr]
                turned[n] = act("xsT", [tr, *last_use["xsT"][r]], nc.scalar.copy, xsT[:, r, :], bank[r][:, 0:P])
                freed[r] = [turned[n]]

            def own_weights(n, which, own, table, landed):
                r = n % 2

                def copy(to):
                    offset = nc.vector.value_load(owner[0:1, u, n:n + 1], min_val=0, max_val=(E - 1) * F)
                    return nc.vector.tensor_copy(to, table[:, bass.DynSlice(offset, F)])

                weights[which, n] = dve(which, [owned, landed, *last_use[which][r]], copy, own[:, r, :])
                last_use["owner"][u] = [weights[which, n]]

            def first(n):
                r = n % 2
                for k in range(FC):
                    mm = pe("first", [turned[n], weights["w1_own", n], *freed[2 + r]], nc.tensor.matmul,
                            bank[2 + r][:, k * P:(k + 1) * P], w1_own[:, r, k * P:(k + 1) * P], xsT[:, r, :],
                            start=k == 0, stop=k == FC - 1, skip_group_check=True)
                last_use["w1_own"][r] = [mm]
                last_use["xsT"][r] = [mm]
                hidden[n] = act("gelu", [mm, *last_use["hidT"][r]], nc.scalar.activation,
                                hidT[:, r, :], bank[2 + r][:], ACT.Gelu)
                freed[2 + r] = [hidden[n]]

            def second(n):
                lot, r = n // LOT, n % 2

                for k in range(FC):
                    mm = pe("second", [hidden[n], weights["w2_own", n], *freed[4 + r]], nc.tensor.matmul,
                            bank[4 + r][:, 0:C], hidT[:, r, k * P:(k + 1) * P], w2_own[:, r, k * C:(k + 1) * C],
                            start=k == 0, stop=k == FC - 1)
                last_use["w2_own"][r] = [mm]
                last_use["hidT"][r] = [mm]
                yd = dve("ys", [mm, *last_use["ys"][lot % 2]], nc.vector.tensor_copy,
                         ys[:, lot % 2, n % LOT, :], bank[4 + r][:, 0:C])
                freed[4 + r] = [yd]
                if n % LOT == LOT - 1:
                    st = Q.add("sync", f"ys{lot % 2}", [yd, *ys_read[u]], 16, nc.sync.dma_start,
                               ys_tiles[:, lot * LOT:(lot + 1) * LOT, :], ys[:, lot % 2, :, :])
                    last_use["ys"][lot % 2] = [st]
                    stored[u].append(st)

            stored[u] = []
            beside = ("xs", "xsT", "w1_own", "w2_own", "hidT")
            for name in beside:
                last_use[name] = [last_use[name][r] + last_use["pt"][0] + last_use["pt"][1] for r in range(2)]
            load(0)
            for n in range(ST + 2):
                for _ in range(-(-len(background) // (ST + 2 - n))):
                    background.pop(0)((6, 7))
                if n < ST:
                    turn(n)
                    own_weights(n, "w1_own", w1_own, w1_flat, got_w1)
                if 0 <= n - 1 < ST:
                    own_weights(n - 1, "w2_own", w2_own, w2_flat, got_w2)
                    first(n - 1)
                if 0 <= n - 2 < ST:
                    second(n - 2)
            xs_read[u] = list(loaded.values())
            last_use["pt"] = [[token for name in beside for uses in last_use[name] for token in uses]] * 2

        def combine(l, u):
            fetched = {}

            def fetch(t):
                r = t % 4
                fetched[t] = [Q.add("gpsimd", f"got{r}", [*stored[u], *last_use["got"][r]], 16,
                                    nc.gpsimd.indirect_dma_start, got[:, r, i, :], None, ys_dram[u],
                                    bass.IndirectOffsetOnAxis(slot[:, u, i, t:t + 1], 0)) for i in range(TOP)]
                last_use["slot"][u] = ys_read[u] = fetched[t]

            def step(t):
                for ahead in range(t, min(t + 3, UT)) if t == 0 else range(t + 2, min(t + 3, UT)):
                    fetch(ahead)
                at, prev = u * UT + t, None
                for i in range(TOP):
                    prev = dve("moe", [*fetched[t], prev], nc.vector.scalar_tensor_tensor,
                               out=x[:, at, :], in0=got[:, t % 4, i, :], scalar=wtop[:, u, i, t],
                               in1=x[:, at, :], op0=ALU.mult, op1=ALU.add)
                last_use["got"][t % 4] = [prev]
                x_ready[at // TB] = [prev]
                if l == 1 and t % 4 == 3:
                    b, tb = at // TB, at % TB
                    stores.append(Q.add("sync", "store", [prev], 16, nc.sync.dma_start,
                                        out_dram[b][:, tb - 3:tb + 1, :], x[:, at - 3:at + 1, :]))

            return [lambda banks, t=t: step(t) for t in range(UT)]

        background, alongside = [], []
        prepared, routed, scattered, stored = {}, {}, {}, {}
        xs_read, ys_read = {u: [] for u in range(U)}, {u: [] for u in range(U)}
        stores = []

        def finish(steps):
            while steps:
                steps.pop(0)((6, 7))

        def route_and_prepare(l, u, next_l, next_b):
            ahead = prepare(next_l, next_b)
            return route(l, u) + ahead[0:2] + [lambda banks: scatter(l, u)] + ahead[2:]

        finish(prepare(0, 0))
        alongside += prepare(0, 1)
        attention(0, 0)
        alongside += prepare(0, 2)
        attention(0, 1)
        alongside += route_and_prepare(0, 0, 0, 3)
        attention(0, 2)
        experts(0, 0)
        background += combine(0, 0)
        alongside += prepare(1, 0)
        attention(0, 3)
        alongside += route_and_prepare(0, 1, 1, 1)
        attention(1, 0)
        experts(0, 1)
        background += combine(0, 1)
        alongside += prepare(1, 2)
        attention(1, 1)
        alongside += route_and_prepare(1, 0, 1, 3)
        attention(1, 2)
        attention(1, 3)
        background += route(1, 1) + [lambda banks: scatter(1, 1)]
        experts(1, 0)
        background += combine(1, 0)
        experts(1, 1)
        finish(combine(1, 1))
        Q.add("sync", "end", stores, 1, nc.sync.drain)

        block = ctx.enter_context(nc.Block())
        Q.play(nc, ctx, block)


def kernel(**inputs):
    import concourse.bacc as bacc
    from concourse.bass_utils import run_bass_kernel_spmd

    a = {k: np.asarray(v) for k, v in inputs.items()}
    def heads(w):
        return w.reshape(*w.shape[:-1], G, J, D).swapaxes(-3, -2).reshape(w.shape)

    masks, picks, table = constants()
    pa, pb = "L0_attn_a_", "L0_attn_b_"
    b_cols = np.stack([heads(a[pb + n]) for n in ("bq", "bk")], axis=1)
    arrays = {
        "x_in": a[pa + "x"],
        "w_a": np.stack([heads(a[pa + n].T) for n in ("Wq", "Wk", "Wv")] + [heads(a[pa + "Wo"]).T]),
        "bo_a": a[pa + "bo"].reshape(1, C),
        "w_b": np.stack([heads(a[pb + n]) for n in ("Wq", "Wk", "Wv")] + [heads(a[pb + "Wo"].T).T]),
        "b_b": np.stack([heads(a[pb + n]) for n in ("bq", "bk", "bv")] + [a[pb + "bo"]]),
        "b_cols_in": b_cols,
        "gate_w": a["L0_ffn_gate_w"],
        "w1": a["L0_ffn_w1"],
        "w2": a["L0_ffn_w2"],
        "masks_in": masks,
        "picks_in": picks,
        "table_in": table,
    }
    nc = bacc.Bacc("TRN2", target_bir_lowering=False, num_devices=1)
    args = []
    for name, arr in arrays.items():
        arrays[name] = np.ascontiguousarray(arr)
        args.append(nc.dram_tensor(name, arr.shape, mybir.dt.from_np(arr.dtype), kind="ExternalInput").ap())
    args.append(nc.dram_tensor("out", (B, S, C), F32, kind="ExternalOutput").ap())
    build(nc, *args)
    return run_bass_kernel_spmd(nc, [arrays], core_ids=[0]).results[0]["out"]
```

```python
from contextlib import ExitStack

import numpy as np

import concourse.bass as bass
from concourse import mybir

F32 = mybir.dt.float32
F32R = mybir.dt.float32r
BF16 = mybir.dt.bfloat16
U32 = mybir.dt.uint32
I32 = mybir.dt.int32
ALU = mybir.AluOpType
ACT = mybir.ActivationFunctionType
AX_X = mybir.AxisListType.X

P = 128
B, S, C = 4, 1024, 128
H, D = 16, 8
J, G = 4, 4
ROWS = P // J
TB = S // P
TT = B * TB
QB = 64
NBLK = S // QB
WIN = 64
PAD = WIN // 2
EXT_A = S + 2 * PAD
KEYS_A = 2 * QB
SPAN_A = P + 2 * PAD
NG = 8
KEYS_B = QB + NG
SPAN_B = 2 * KEYS_B
EXT_B = NBLK * KEYS_B
GLOBALS = [int(v) for v in np.linspace(0, S - 1, NG).astype(np.int64)]
E, F = 8, 512
FC = F // P
U = 2
UT = TT // U
TOP = 2
ST = UT * TOP + E - 1
LOT = 3
assert ST % LOT == 0
SCALE = float(D) ** -0.5
EPS = 1e-5
MASKED = -1e30


def constants():
    q, k = (np.arange(P) % QB)[:, None], np.arange(KEYS_A)[None, :]
    window = np.where((k >= q) & (k < q + WIN), 0.0, MASKED)
    q, k = np.arange(P)[:, None], np.arange(SPAN_A)[None, :]
    tile_window = np.where((k >= q) & (k < q + WIN), 0.0, MASKED)
    own_keys, own_queries = np.arange(EXT_B) // KEYS_B, np.arange(S) // QB
    patterns = np.zeros((P, EXT_B + S + P))
    for i, pos in enumerate(GLOBALS):
        patterns[0, pos // QB * KEYS_B + QB + i] = MASKED
    patterns[0, EXT_B:EXT_B + S] = 1
    for half in range(2):
        patterns[1 + half, 0:EXT_B] = np.where(own_keys % 2 == half, 0.0, MASKED)
        patterns[1 + half, EXT_B:EXT_B + S] = own_queries % 2 == half
    for i in range(3):
        patterns[i, EXT_B + S + 3 * D + 1 + i::ROWS] = 1
    masks = np.concatenate([tile_window, window, np.eye(P), patterns], axis=1)
    chan, row = np.arange(P)[:, None], np.arange(P)[None, :]
    same = (chan // ROWS == row // ROWS) & (chan % D == row % D)
    product = row % ROWS // D
    picks = np.zeros((P, 2, 2, G, P))
    for g in range(G):
        own = same & (chan // D % G == g)
        picks[:, 0, 0, g] = own & ((product == 0) | (product == 2))
        picks[:, 0, 1, g] = own & (product == 1)
        picks[:, 1, 0, g] = own & ((product == 0) | (product == 1))
        picks[:, 1, 1, g] = own & (product == 2)
    cols = np.zeros((P, 2), np.float32)
    cols[:, 1] = np.arange(P) % ROWS == 3 * D
    heads = np.zeros((P, H), np.float32)
    heads[np.arange(P), 4 * ((np.arange(P) // D) % G) + np.arange(P) // ROWS] = 1
    stack = np.zeros((P, G), np.float32)
    stack[np.arange(P), (np.arange(P) // D) % G] = 1
    sums = np.broadcast_to(np.repeat(np.eye(G), D, axis=1).reshape(1, G * ROWS), (P, G * ROWS))
    before = (np.arange(P)[:, None] < np.arange(P)[None, :]).astype(np.float32)
    slot_tiles = np.tile(np.arange(ST, dtype=np.float32), (P, 1))
    experts = np.tile(np.arange(E, dtype=np.float32), (P, 1))
    table = np.concatenate([np.eye(P, dtype=np.float32), cols, heads, stack, experts, sums, before, slot_tiles],
                           axis=1)
    return masks.astype(np.float32), picks.reshape(P, -1).astype(np.float32), np.ascontiguousarray(table.astype(np.float32))


class Token:

    def __init__(self, sem_name, amount):
        self.sem_name, self.amount, self.waited, self.value = sem_name, amount, False, None


class Queues:

    ENGINES = ("sync", "tensor", "vector", "scalar", "gpsimd")

    def __init__(self):
        self.steps = {e: [] for e in self.ENGINES}

    def add(self, engine, stage, after, amount, instruction, *operands, **options):
        token = Token(f"{engine}_{stage}", amount)
        self.steps[engine].append((instruction, operands, options, after, token))
        return token

    def play(self, nc, ctx, block):
        for steps in self.steps.values():
            for _, _, _, after, _ in steps:
                for token in after:
                    if token is not None:
                        token.waited = True
        sems, count = {}, {}
        for engine in self.ENGINES:
            for *_, token in self.steps[engine]:
                if token.waited:
                    name = token.sem_name
                    if name not in sems:
                        sems[name] = ctx.enter_context(nc.semaphore(name))
                    count[name] = count.get(name, 0) + token.amount
                    token.value = count[name]

        def run(engine):
            def body(eng):
                reached = {}
                for instruction, operands, options, after, token in self.steps[engine]:
                    need = {}
                    for t in after:
                        if t is not None:
                            need[t.sem_name] = max(need.get(t.sem_name, 0), t.value)
                    for name, value in need.items():
                        if reached.get(name, 0) < value:
                            eng.wait_ge(sems[name], value)
                            reached[name] = value
                    ins = instruction(*operands, **options)
                    if token.waited:
                        ins.then_inc(sems[token.sem_name], token.amount)
            return body

        block.sync(run("sync"))
        block.tensor(run("tensor"))
        block.vector(run("vector"))
        block.scalar(run("scalar"))
        block.gpsimd(run("gpsimd"))


def build(nc, x_in, w_a, bo_a, w_b, b_b, b_cols_in, gate_w, w1, w2, masks_in, picks_in, table_in, out):
    Q = Queues()

    def pe(stage, after, instruction, *operands, **options):
        return Q.add("tensor", stage, after, 1, instruction, *operands, **options)

    def dve(stage, after, instruction, *operands, **options):
        return Q.add("vector", stage, after, 1, instruction, *operands, **options)

    def act(stage, after, instruction, *operands, **options):
        return Q.add("scalar", stage, after, 1, instruction, *operands, **options)

    def pool(stage, after, instruction, *operands, **options):
        return Q.add("gpsimd", stage, after, 1, instruction, *operands, **options)

    n_dma = [0]

    def dma(name, dst, src, *after):
        n_dma[0] += 1
        return Q.add("sync", f"{name}_{n_dma[0]}", after, 16, nc.sync.dma_start, dst, src)

    with ExitStack() as ctx:
        def sb(name, shape, dt=F32):
            return ctx.enter_context(nc.sbuf_tensor(name, shape, dt))

        x = sb("x", [P, TT, C])
        xn = sb("xn", [P, TB, C])
        ext = sb("ext", [P, EXT_B])
        kst = sb("kst", [P, G, EXT_B], F32R)
        qst = sb("qst", [P, G, S], F32R)
        planes = sb("planes", [P, 2, G, J, SPAN_A], F32R)
        hi = sb("hi", [P, 2, 512], F32R)
        lo = sb("lo", [P, 2, 512], F32R)
        picks = sb("picks", [P, 2, 2, G, P], F32R)
        v = sb("v", [P, NBLK, C])
        pt = sb("pt", [P, 2, G, J * P])
        rden = sb("rden", [P, 2, P])
        on = sb("on", [P, 2, P])
        mx = sb("mx", [P, J, G, TB])
        mxT = sb("mxT", [P, P], F32R)
        w_attn = [sb(f"w_attn{l}", [P, 4, C]) for l in range(2)]
        b_nat = sb("b_nat", [P, 3, C])
        b_cols = sb("b_cols", [P, 2])
        gate = sb("gate", [P, E])
        w1_sb = sb("w1_sb", [P, E, F])
        w2_sb = sb("w2_sb", [P, E, FC, C])
        masks = sb("masks", [P, SPAN_A + KEYS_A + P], BF16)
        patterns = sb("patterns", [3, EXT_B + S + P], BF16)
        table = sb("table", [P, P + 2 + H + G + E + G * ROWS + P + ST])
        power = sb("power", [P, TB])
        stats = sb("stats", [P, TB, 6])
        mv = sb("mv", [P, TB, 2])
        veps = sb("veps", [P, TB])
        rstd = sb("rstd", [P, TB])
        gq = sb("gq", [P, NG])
        gbd = sb("gbd", [P, H, NG])
        gp = sb("gp", [P, S])
        gs = sb("gs", [P, 4])
        turned = sb("turned", [P, NBLK * P])
        gpT = turned[0:QB, :].rearrange("p (n q) -> p n q", q=P)
        gsel = sb("gsel", [P, H, NG])
        gout = sb("gout", [P, NG])
        fxn = sb("fxn", [P, UT, C])
        gT = turned[:, 0:2 * 512].rearrange("p (r n) -> p r n", r=2)
        logits = sb("logits", [P, UT, E])
        top = sb("top", [P, UT, 8])
        topi = sb("topi", [P, UT, 8], U32)
        topf = sb("topf", [P, UT, TOP])
        wdif = sb("wdif", [P, UT, 1])
        wexp = sb("wexp", [P, UT, 1])
        wsum = sb("wsum", [P, UT, 1])
        wtop = sb("wtop", [P, U, TOP, UT, 1])
        hot = sb("hot", [P, TOP, UT, E])
        both = sb("both", [P, UT, E])
        whole = sb("whole", [P, UT, E])
        upto = sb("upto", [P, UT, E])
        rank = sb("rank", [P, UT, E])
        ones = sb("ones", [P, P])
        n_int = sb("n_int", [P, 2, E], U32)
        n_flt = sb("n_flt", [P, 3, E])
        hit = sb("hit", [P, UT, E])
        slot_f = sb("slot_f", [P, TOP, UT])
        slot = sb("slot", [P, U, TOP, UT], U32)
        passed = sb("passed", [1, ST, E])
        owner_f = sb("owner_f", [1, 2, ST])
        owner = sb("owner", [1, U, ST], I32)
        shared, at = pt[:].rearrange("p r g n -> p (r g n)"), 0
        tile_views = []
        for n in (LOT * C, P, F, F, F):
            tile_views.append(shared[:, at:at + 2 * n].rearrange("p (r n) -> p r n", r=2))
            at += 2 * n
        xs, xsT, w1_own, w2_own, hidT = tile_views
        xs = xs.rearrange("p r (n c) -> p r n c", c=C)
        ys = sb("ys", [P, 2, LOT, C])
        got = sb("got", [P, 4, TOP, C])

        xs_dram = [nc.dram_tensor(f"xs_dram{u}", (ST * P, C), F32, kind="Internal").ap() for u in range(U)]
        ys_dram = [nc.dram_tensor(f"ys_dram{u}", (ST * P, C), F32, kind="Internal").ap() for u in range(U)]

        bank = [ctx.enter_context(nc.psum_tensor(f"bank{i}", [P, 512], F32)) for i in range(8)]
        freed = [[] for _ in range(8)]

        tile_window, window = masks[:, 0:SPAN_A], masks[:, SPAN_A:SPAN_A + KEYS_A]
        eye16 = masks[:, SPAN_A + KEYS_A:]
        pattern_of = patterns[:, EXT_B:EXT_B + S], patterns[:, 0:EXT_B]
        into_rows = patterns[:, EXT_B + S:]
        eye = table[:, 0:P]
        no_bias, k_one = table[:, P:P + 1], table[:, P + 1:P + 2]
        at = P + 2
        table_ap = []
        for n in (H, G, E, G * ROWS, P, ST):
            table_ap.append(table[:, at:at + n])
            at += n
        head_of, stack_of, iota_e, stack_sums, before, iota_s = table_ap
        stack_sums = stack_sums.rearrange("p (g c) -> p g c", g=G)

        x_dram = x_in.rearrange("b (t p) c -> b p t c", p=P)
        out_dram = out.rearrange("b (t p) c -> b p t c", p=P)
        got_x = [dma("x", x[:, 0:TB, :], x_dram[0])]
        got_table = dma("table", table[:], table_in)
        got_cols = dma("bcols", b_cols[:], b_cols_in)
        got_w = [dma("wa", w_attn[0][:], w_a.rearrange("m c e -> c m e"))]
        staged = pt[:, 0].rearrange("p g n -> p (g n)")
        n_mask, n_pattern = masks.shape[1], patterns.shape[1]
        masks_landed = dma("masks", staged[:, 0:n_mask], masks_in[:, 0:n_mask])
        staged_picks = pt[:, 1].rearrange("p g n -> p (g n)")
        picks_landed = dma("picks", staged_picks, picks_in)
        staged_patterns = [(fxn[0:3].rearrange("p t c -> p (t c)")[:, 0:EXT_B], slice(0, EXT_B)),
                           (v[0:3].rearrange("p n c -> p (n c)")[:, 0:S + P], slice(EXT_B, n_pattern))]
        patterns_landed = [dma("patterns", to, masks_in[0:3, n_mask + part.start:n_mask + part.stop])
                           for to, part in staged_patterns]
        got_x += [dma("x", x[:, b * TB:(b + 1) * TB, :], x_dram[b]) for b in range(1, B)]
        got_bo = [dma("bo", b_nat[:, 0, :], bo_a.broadcast_to([P, C]))]
        got_gate = dma("gate", gate[:], gate_w)
        got_w1 = dma("w1", w1_sb[:], w1.rearrange("e c f -> c e f"))
        got_w2 = dma("w2", w2_sb[:], w2.rearrange("e (k f) c -> f e k c", f=P))
        got_w.append(dma("wb", w_attn[1][:], w_b.rearrange("m c e -> c m e")))
        got_bo.append(dma("bo", b_nat[:, 1, :], b_b[3:4, :].broadcast_to([P, C])))
        got_bias = dma("bv", b_nat[:, 2, :], b_b[2:3, :].broadcast_to([P, C]))

        ones_set = dve("ones", [], nc.vector.memset, ones[:], 1.0)
        blank = dve("blank", [], nc.vector.memset, planes[:].rearrange("p r g j k -> p (r g j k)").bitcast(F32), 0.0)
        zeros, n_zeros = turned[:], NBLK * P
        zeros_set = dve("zeros", [], nc.vector.memset, zeros, 0.0)
        slots_of = [xs_dram[u].rearrange("(p n) c -> p (n c)", p=P) for u in range(U)]
        zeroed = [[Q.add("sync", f"zeroed{u}", [zeros_set], 16, nc.sync.dma_start,
                         slots_of[u][:, at:min(at + n_zeros, ST * C)], zeros[:, 0:min(n_zeros, ST * C - at)])
                   for at in range(0, ST * C, n_zeros)] for u in range(U)]
        power_set = dve("power", [], nc.vector.memset, power[:], -0.5)
        got_masks = dve("masks", [masks_landed], nc.vector.tensor_copy, masks[:], staged[:, 0:n_mask])
        for landed, (staged_part, part) in zip(patterns_landed, staged_patterns):
            got_patterns = dve("patterns", [landed], nc.vector.tensor_copy, patterns[:, part], staged_part)
        got_picks = act("picks", [picks_landed], nc.scalar.copy, picks[:].rearrange("p m h g n -> p (m h g n)"), staged_picks)
        x_ready = [[got_x[b]] for b in range(B)]

        def moments(b):
            for t in range(TB):
                st = dve("bn", [*x_ready[b]], nc.vector.bn_stats, stats[:, t, :], x[:, b * TB + t, :])
            for t in range(TB):
                ag = dve("agg", [st], nc.vector.bn_aggr, mv[:, t, :], stats[:, t, :])
            ve = dve("veps", [ag, *rstd_read], nc.vector.tensor_scalar, veps[:], mv[:, :, 1], EPS, None, ALU.add)
            rstd_set[:] = [pool("rstd", [ve, power_set], nc.gpsimd.tensor_tensor,
                                rstd[:], veps[:], power[:], ALU.pow)]

        def norm(b, to, to_free):
            done = [dve("norm", [*rstd_set, *to_free], nc.vector.tensor_scalar,
                        to[:, t, :], x[:, b * TB + t, :], mv[:, t, 0:1], rstd[:, t:t + 1], ALU.subtract, ALU.mult)
                    for t in range(TB)]
            rstd_read[:] = [done[-1]]
            return done

        rstd_set, rstd_read, xn_read = [], [], []

        def turn_tokens(chunk, normed, banks, dst, dst_free):
            bk = banks[chunk % 2]
            for t in range(4 * chunk, 4 * chunk + 4):
                tr = pe("xT", [normed[t], got_table, *freed[bk]], nc.tensor.transpose,
                        bank[bk][:, (t % 4) * P:(t % 4 + 1) * P], xn[:, t, :], eye)
            freed[bk] = [act("xT", [tr, *dst_free], nc.scalar.copy,
                             dst, bank[bk][:].rearrange("p (n q) -> p n q", q=QB))]
            xn_read[:] = [tr]
            return freed[bk][0]

        last_use = {name: [] for name in ("ext", "kst", "qst", "mxT", "wexp")}
        last_use |= {name: [[], []] for name in ("on", "hi", "slot", "owner", "xs", "xsT", "w1_own", "w2_own",
                                                 "hidT", "ys")}
        last_use |= {"got": [[], [], [], []], "v": [got_patterns], "fxn": [got_patterns],
                     "planes": [[blank], [blank]], "pt": [[got_masks], [got_picks]],
                     "gT": [zeroed[0] + zeroed[1]] * 2}

        def ext_body(l, c):
            if l == 0:
                return ext[:, PAD + 512 * c:PAD + 512 * c + 512].rearrange("p (n q) -> p n q", q=QB)
            return ext[:, 0:EXT_B].rearrange("p (n k) -> p n k", k=KEYS_B)[:, 8 * c:8 * c + 8, 0:QB]

        def prepare(l, b):
            normed, copies = [], []

            def turn(chunk):
                return lambda banks: copies.append(
                    turn_tokens(chunk, normed, banks, ext_body(l, chunk), last_use["ext"]))

            def edges(banks):
                ext_full = list(copies)
                if l == 0:
                    ext_full.append(dve("edge", [copies[0]], nc.vector.tensor_copy,
                                        ext[:, 0:PAD], ext[:, PAD:PAD + 1].broadcast_to([P, PAD])))
                    ext_full.append(dve("edge", [copies[1]], nc.vector.tensor_copy, ext[:, PAD + S:EXT_A],
                                        ext[:, PAD + S - 1:PAD + S].broadcast_to([P, PAD])))
                else:
                    blocks = ext[:, 0:EXT_B].rearrange("p (n k) -> p n k", k=KEYS_B)
                    for i, pos in enumerate(GLOBALS):
                        src = (pos // QB) * KEYS_B + pos % QB
                        ext_full.append(dve("edge", [copies[pos // 512]], nc.vector.tensor_copy,
                                            blocks[:, :, QB + i], ext[:, src:src + 1].broadcast_to([P, NBLK])))
                prepared[l, b] = normed, ext_full

            return [lambda banks: moments(b), lambda banks: normed.extend(norm(b, xn, xn_read)),
                    *(turn(c) for c in range(TB // 4)), edges]

        def attention(l, b):
            keys, ext_n, span = ((KEYS_A, EXT_A, SPAN_A), (KEYS_B, EXT_B, SPAN_B))[l]
            step = (QB, KEYS_B)[l]
            normed, ext_full = prepared[l, b]
            chunks = [(0, 512 * c, 512, ext_body(l, c) if l else ext[:, PAD + 512 * c:PAD + 512 * c + 512])
                      for c in range(S // 512)]
            chunks += [(1, at, min(512, ext_n - at), ext[:, at:min(at + 512, ext_n)]) for at in range(0, ext_n, 512)]

            def plain(i):
                m, at, n, view = chunks[i]
                bk, r = 4 + i % 2, i % 2
                bias = b_cols[:, m:m + 1] if l else no_bias
                mm = pe("proj", [got_w[l], *ext_full, *freed[bk]], nc.tensor.matmul,
                        bank[bk][:, 0:n], w_attn[l][:, m, :], view, start=True, stop=True)
                hd = act("hi", [mm, got_cols, got_table, *last_use["hi"][r]], nc.scalar.activation,
                         hi[:, r, 0:n], bank[bk][:, 0:n], ACT.Identity, bias=bias)
                ld = dve("lo", [hd], nc.vector.scalar_tensor_tensor,
                         out=lo[:, r, 0:n], in0=bank[bk][:, 0:n], scalar=bias, in1=hi[:, r, 0:n].bitcast(F32),
                         op0=ALU.add, op1=ALU.subtract)
                freed[bk] = [ld]
                return ld

            def spread(i, split):
                m, at, n, _ = chunks[i]
                r, dst = i % 2, (qst, kst)[m]
                ones_of = k_one if m else no_bias
                done = []
                for g in range(G):
                    pe("spread", [split, got_picks, *freed[g]], nc.tensor.matmul,
                       bank[g][:, 0:n], picks[:, m, 0, g, :], hi[:, r, 0:n], start=True, stop=False)
                    mm = pe("spread", [], nc.tensor.matmul,
                            bank[g][:, 0:n], picks[:, m, 1, g, :], lo[:, r, 0:n], start=False,
                            stop=l == 0)
                    if l == 1:
                        mm = pe("spread", [got_patterns], nc.tensor.matmul, bank[g][:, 0:n], into_rows,
                                pattern_of[m][:, at:at + n], start=False, stop=True)
                    free = last_use[("qst", "kst")[m]]
                    if g % 2:
                        cp = act("spread", [mm, *free], nc.scalar.activation,
                                 dst[:, g, at:at + n], bank[g][:, 0:n], ACT.Identity,
                                 bias=ones_of)
                    else:
                        cp = dve("spread", [mm, *free], nc.vector.tensor_scalar,
                                 dst[:, g, at:at + n], bank[g][:, 0:n], ones_of, None, ALU.add)
                    freed[g] = [cp]
                    done.append(cp)
                last_use["hi"][r] = [mm]
                return done[-2:]

            split, stacks_set = plain(0), [None, None]
            for i in range(len(chunks)):
                ahead = plain(i + 1) if i + 1 < len(chunks) else None
                stacks_set[chunks[i][0]] = spread(i, split)
                split = ahead
            q_set, k_set = stacks_set
            g_steps, g_outputs = global_queries() if l else ([], None)

            def key_planes(t):
                copies, first = [], t * P if l == 0 else 2 * t * KEYS_B
                for j in range(J):
                    r = slice(j * ROWS, (j + 1) * ROWS)
                    queue, copy = ((dve, nc.vector.tensor_copy) if t < 2 and j % 2 else (act, nc.scalar.copy))
                    copies.append(queue("planes", [*k_set, *last_use["planes"][t % 2]], copy,
                                        planes[r, t % 2, :, j, 0:span], kst[r, :, first:first + span]))
                return copies

            filled = {t: key_planes(t) for t in range(2)}
            for t in range(TB):
                for _ in range(-(-len(g_steps) // (TB - t))):
                    g_steps.pop(0)((6, 7))
                for n in range(G * J // 2):
                    g, j, bk = n // 2, n % 2 * 2, (G * J // 2 * t + n) % 6
                    if l == 0:
                        pe("mmask", [got_masks, *freed[bk]], nc.tensor.matmul, bank[bk][:, 0:2 * span], eye16,
                           tile_window.rearrange("p (o k) -> p o k", o=1).broadcast_to([P, 2, span]),
                           start=True, stop=False, skip_group_check=True)
                    mm = pe("mscore", [*q_set, *filled[t], *freed[bk]], nc.tensor.matmul,
                            bank[bk][:, 0:2 * span], qst[:, g, t * P:(t + 1) * P],
                            planes[:, t % 2, g, j:j + 2, 0:span], start=l == 1, stop=True, skip_group_check=True)
                    md = dve("max", [mm], nc.vector.reduce_max, mx[:, j:j + 2, g, t],
                             bank[bk][:, 0:2 * span].rearrange("p (j k) -> p j k", j=2), AX_X)
                    freed[bk] = [md]
                last_use["planes"][t % 2] = [mm]
                if t + 2 < TB:
                    filled[t + 2] = key_planes(t + 2)
            tr = pe("mT", [md, *freed[7]], nc.tensor.transpose,
                    bank[7][:, 0:P], mx[:].rearrange("p j g t -> p (j g t)"), eye)
            neg = dve("neg", [tr, *last_use["mxT"]], nc.vector.tensor_scalar,
                      mxT[:], bank[7][:, 0:P], -1.0, None, ALU.mult)
            freed[7] = [neg]
            rows = []
            for j in range(J):
                row = qst[j * ROWS + 3 * D:j * ROWS + 3 * D + 1, :, :].rearrange("o g s -> o (g s)")
                rows.append(Q.add("sync", "mrow", [neg, mm], 16, nc.sync.dma_start,
                                  row.rearrange("o (r q) -> o r q", q=P).bitcast(F32),
                                  mxT[G * TB * j:G * TB * (j + 1), :].bitcast(F32)))
            last_use["mxT"] = rows

            for c in range(NBLK // 4):
                bk = 6 + c % 2
                for i in range(4):
                    blk = 4 * c + i
                    mm = pe("v", [got_w[l], *ext_full, *freed[bk]], nc.tensor.matmul,
                            bank[bk][0:keys, i * C:(i + 1) * C], ext[:, blk * step:blk * step + keys],
                            w_attn[l][:, 2, :], start=i == 0, stop=i == 3, skip_group_check=True)
                src = bank[bk][0:keys, :].rearrange("p (n c) -> p n c", c=C)
                if l == 0:
                    v_set = act("v", [mm, *last_use["v"]], nc.scalar.copy, v[0:keys, 4 * c:4 * c + 4, :], src)
                else:
                    v_set = dve("v", [mm, got_bias, *last_use["v"]], nc.vector.tensor_tensor,
                                v[0:keys, 4 * c:4 * c + 4, :], src,
                                b_nat[0:keys, 2:3, :].broadcast_to([keys, 4, C]), ALU.add)
                freed[bk] = [v_set]
            last_use["ext"] = [mm]
            g_done = g_outputs((6, 7), v_set) if l else []

            beside(-1, (6, 7))
            biased = pool("bo", [*normed, got_bo[l]], nc.gpsimd.tensor_tensor,
                          x[:, b * TB:(b + 1) * TB, :], x[:, b * TB:(b + 1) * TB, :],
                          b_nat[:, l:l + 1, :].broadcast_to([P, TB, C]), ALU.add)

            slotted = {}

            def slots(t):
                slotted[t] = []
                for j in range(J):
                    r = slice(j * ROWS, (j + 1) * ROWS)
                    queue, copy = ((dve, nc.vector.tensor_copy), (act, nc.scalar.copy))[j % 2]
                    slotted[t].append(queue("slots", [*rows, *last_use["planes"][t % 2]], copy,
                                            planes[r, t % 2, :, j, 0:P], qst[r, :, t * P:(t + 1) * P]))

            def numerators(t):
                r2 = t % 2
                for g in range(G if l == 0 else 0):
                    pe("emask", [*freed[g]], nc.tensor.matmul,
                       bank[g][:], window, eye16.rearrange("p (o q) -> p o q", o=1).broadcast_to([P, J, P]),
                       start=True, stop=False, skip_group_check=True)
                exps = []
                for g in range(G):
                    for h in range(2):
                        blk = 2 * t + h
                        mm = pe("escore", [*slotted[t], *freed[g]], nc.tensor.matmul,
                                bank[g][0:keys, :].rearrange("p (j b q) -> p j b q", j=J, b=2)[:, :, h, :],
                                kst[:, g, blk * step:blk * step + keys], planes[:, r2, g, :, h * QB:(h + 1) * QB],
                                start=l == 1 and h == 0, stop=h == 1, skip_group_check=True)
                    exps.append(act("exp", [mm, *last_use["pt"][r2]], nc.scalar.activation,
                                    pt[0:keys, r2, g, :], bank[g][0:keys, :], ACT.Exp, scale=SCALE))
                    freed[g] = [exps[g]]
                last_use["planes"][r2] = [mm]
                return exps

            def values(t, exps):
                r2 = t % 2
                nb, db = 4 + 2 * r2, 5 + 2 * r2
                num, den = bank[nb], bank[db]
                for j in range(J):
                    c = slice(j * ROWS, (j + 1) * ROWS)
                    for g in range(G):
                        mm = pe("den", [exps[g], got_table, *freed[db]], nc.tensor.matmul,
                                den[c, 0:P], stack_sums[0:keys, g, :], pt[0:keys, r2, g, j * P:(j + 1) * P],
                                start=g == 0, stop=g == G - 1, skip_group_check=True, tile_position=(0, c.start))
                rc = dve("rden", [mm], nc.vector.reciprocal, rden[:, r2, :], den[:, 0:P])
                freed[db] = [rc]
                for h in range(2):
                    for j in range(J):
                        c = slice(j * ROWS, (j + 1) * ROWS)
                        pcol = pt[0:keys, r2, :, j * P + h * QB:j * P + (h + 1) * QB]
                        ncol = num[c, :].rearrange("p (g b q) -> p g b q", g=G, b=2)[:, :, h, :]
                        mm = pe("pv", [v_set, *freed[nb]], nc.tensor.matmul,
                                ncol, v[0:keys, 2 * t + h, c], pcol, start=h == 0, stop=h == 1,
                                skip_group_check=True, tile_position=(0, c.start))
                last_use["pt"][r2] = [mm]
                on_set = None
                for g in range(G):
                    stack = num[:, g * P:(g + 1) * P], stack_of[:, g:g + 1]
                    if g == 0:
                        on_set = dve("own", [mm, *last_use["on"][r2]], nc.vector.tensor_scalar,
                                     on[:, r2, :], *stack, None, ALU.mult)
                    else:
                        on_set = dve("own", [on_set], nc.vector.scalar_tensor_tensor, on[:, r2, :], *stack,
                                     on[:, r2, :], ALU.mult, ALU.add)
                freed[nb] = [on_set]
                on_set = dve("on", [on_set, rc], nc.vector.tensor_tensor,
                             on[:, r2, :], on[:, r2, :], rden[:, r2, :], ALU.mult)
                for i, pos in enumerate(GLOBALS if l else []):
                    if pos // P == t:
                        on_set = dve("gput", [on_set, *g_done], nc.vector.tensor_copy,
                                     on[:, r2, pos % P:pos % P + 1], gout[:, i:i + 1])
                return mm, on_set

            def output(t, on_set):
                r2 = t % 2
                nb = 4 + 2 * r2
                wo = pe("wo", [on_set, got_w[l]], nc.tensor.matmul,
                        bank[nb][:, 0:C], on[:, r2, :], w_attn[l][:, 3, :], start=True, stop=True)
                last_use["on"][r2] = [wo]
                rs = dve("resid", [wo, biased], nc.vector.tensor_tensor,
                         x[:, b * TB + t, :], x[:, b * TB + t, :], bank[nb][:, 0:C], ALU.add)
                freed[nb] = [rs]
                return rs

            slots(0)
            slots(1)
            exps, on_set = numerators(0), None
            for t in range(TB):
                ahead = numerators(t + 1) if t + 1 < TB else None
                if t + 2 < TB:
                    slots(t + 2)
                mm, on_next = values(t, exps)
                if on_set:
                    output(t - 1, on_set)
                exps, on_set = ahead, on_next
                other = 6 - 2 * (t % 2)
                beside(t, (other, other + 1))
            rs = output(TB - 1, on_set)
            last_use["kst"] = last_use["qst"] = last_use["v"] = [mm]
            x_ready[b] = [rs]

        def global_queries():
            seen = {}
            own_head = head_of.rearrange("p (h o) -> p h o", o=1).broadcast_to([P, H, NG])

            def keys_of_all(banks):
                for c in range(S // 512):
                    bk = banks[c]
                    src = ext[:, 0:EXT_B].rearrange("p (n k) -> p n k", k=KEYS_B)[:, 8 * c:8 * c + 8, 0:QB]
                    mm = pe("gk", [*freed[bk]], nc.tensor.matmul,
                            bank[bk][:], w_attn[1][:, 1, :], src, start=True, stop=True)
                    seen["k"] = act("gk", [mm, got_cols], nc.scalar.activation,
                                    gp[:, 512 * c:512 * c + 512], bank[bk][:], ACT.Identity, bias=b_cols[:, 1:2])
                    freed[bk] = [seen["k"]]

            def queries(banks):
                bk = banks[0]
                mm = pe("gq", [*freed[bk]], nc.tensor.matmul,
                        bank[bk][:, 0:NG], w_attn[1][:, 0, :], ext[:, QB:KEYS_B], start=True, stop=True)
                last_use["ext"] = [mm]
                gqd = dve("gq", [mm, got_cols], nc.vector.tensor_scalar,
                          gq[:], bank[bk][:, 0:NG], b_cols[:, 0:1], None, ALU.add)
                freed[bk] = [gqd]
                seen["q"] = dve("gbd", [gqd], nc.vector.tensor_tensor,
                                gbd[:], gq[:].rearrange("p (o n) -> p o n", o=1).broadcast_to([P, H, NG]),
                                own_head, ALU.mult)

            def scores(banks):
                for c, bk in enumerate(banks):
                    mm = pe("gs", [seen["q"], seen["k"], *freed[bk]], nc.tensor.matmul, bank[bk][:],
                            gbd[:].rearrange("p h n -> p (h n)"), gp[:, 512 * c:512 * c + 512],
                            start=True, stop=True)
                    g1 = dve("gmax", [mm], nc.vector.reduce_max, gs[:, c:c + 1], bank[bk][:], AX_X)
                g2 = dve("gmax", [g1], nc.vector.tensor_tensor, gs[:, 2:3], gs[:, 0:1], gs[:, 1:2], ALU.max)
                g3 = dve("gmax", [g2], nc.vector.tensor_scalar, gs[:, 3:4], gs[:, 2:3], -SCALE, None, ALU.mult)
                for c, bk in enumerate(banks):
                    seen["exp"] = act("gexp", [g3], nc.scalar.activation,
                                      gp[:, 512 * c:512 * c + 512], bank[bk][:], ACT.Exp, bias=gs[:, 3:4],
                                      scale=SCALE)
                    freed[bk] = [seen["exp"]]

            def quotients(banks):
                g4 = dve("gsum", [seen["exp"]], nc.vector.reduce_sum, gs[:, 0:1], gp[:], AX_X)
                g5 = dve("gsum", [g4], nc.vector.reciprocal, gs[:, 1:2], gs[:, 0:1])
                seen["p"] = dve("gnorm", [g5], nc.vector.tensor_scalar, gp[:], gp[:], gs[:, 1:2], None, ALU.mult)

            def turn(c):
                def do(banks):
                    bk = banks[c % 2]
                    for i in range(4):
                        n = 4 * c + i
                        tr = pe("gpT", [seen["p"], *freed[bk]], nc.tensor.transpose,
                                bank[bk][0:QB, i * P:(i + 1) * P], gp[:, n * QB:(n + 1) * QB], eye)
                    seen["turned"] = act("gpT", [tr], nc.scalar.copy, gpT[:, 4 * c:4 * c + 4, :],
                                         bank[bk][0:QB, :].rearrange("p (n q) -> p n q", q=P))
                    freed[bk] = [seen["turned"]]
                return do

            def outputs(banks, v_set):
                bk = banks[0]
                for n in range(NBLK):
                    mm = pe("gpv", [seen["turned"], v_set, *freed[bk]], nc.tensor.matmul,
                            bank[bk][:, 0:P], v[0:QB, n, :], gpT[:, n, :], start=n == 0, stop=n == NBLK - 1)
                sl = dve("gsel", [mm], nc.vector.tensor_tensor,
                         gsel[:], bank[bk][:, 0:P].rearrange("p (h n) -> p h n", h=H), own_head, ALU.mult)
                freed[bk] = [sl]
                return [dve("gout", [sl], nc.vector.reduce_sum, gout[:], gsel[:].rearrange("p h n -> p n h"), AX_X)]

            return [keys_of_all, queries, scores, quotients, *(turn(c) for c in range(NBLK // 4))], outputs

        def route(l, u):
            normed, seen = [], {}

            def norm_to_fxn(n):
                b = u * B // U + n
                return [lambda banks: moments(b),
                        lambda banks: normed.extend(norm(b, fxn[:, n * TB:(n + 1) * TB, :], last_use["fxn"]))]

            def turn(c):
                def do(banks):
                    bk, r = banks[0], c % 2
                    for t in range(4 * c, 4 * c + 4):
                        tr = pe("gT", [normed[t], *freed[bk]], nc.tensor.transpose,
                                bank[bk][:, (t % 4) * P:(t % 4 + 1) * P], fxn[:, t, :], eye)
                    seen["turned", c] = act("gT", [tr, *last_use["gT"][r]], nc.scalar.copy, gT[:, r, :], bank[bk][:])
                    freed[bk] = [seen["turned", c]]
                return do

            def gates(c):
                def do(banks):
                    bk, r = banks[1], c % 2
                    for t in range(4):
                        mm = pe("gate", [seen["turned", c], got_gate, *freed[bk]], nc.tensor.matmul,
                                bank[bk][:, t * E:(t + 1) * E], gT[:, r, t * P:(t + 1) * P], gate[:],
                                start=t == 0, stop=t == 3, skip_group_check=True)
                    last_use["gT"][r] = [mm]
                    lg = dve("gate", [mm], nc.vector.tensor_copy, logits[:, 4 * c:4 * c + 4, :],
                             bank[bk][:, 0:4 * E].rearrange("p (t n) -> p t n", t=4))
                    freed[bk] = [lg]
                    for t in range(4 * c, 4 * c + 4):
                        tp = dve("top", [lg], nc.vector.max, top[:, t, :], logits[:, t, :])
                    for t in range(4 * c, 4 * c + 4):
                        seen["top"] = dve("topi", [tp], nc.vector.max_index,
                                          topi[:, t, :], top[:, t, :], logits[:, t, :])
                return do

            def weigh(banks):
                ti = seen["top"]
                tf = dve("topf", [ti], nc.vector.tensor_copy, topf[:], topi[:, :, 0:TOP])
                wd = dve("wdif", [ti, *last_use["wexp"]], nc.vector.tensor_tensor,
                         wdif[:], top[:, :, 1:2], top[:, :, 0:1], ALU.subtract)
                we = act("wexp", [wd], nc.scalar.activation, wexp[:], wdif[:], ACT.Exp)
                iota3 = iota_e.rearrange("p (o n) -> p o n", o=1).broadcast_to([P, UT, E])
                for i in range(TOP):
                    ho = dve("hot", [tf, got_table], nc.vector.tensor_tensor,
                             hot[:, i], iota3, topf[:, :, i:i + 1].broadcast_to([P, UT, E]), ALU.is_equal)
                seen["both"] = dve("both", [ho], nc.vector.tensor_tensor, both[:], hot[:, 0], hot[:, 1], ALU.add)
                ws = dve("wsum", [we], nc.vector.tensor_scalar, wsum[:], wexp[:], 1.0, None, ALU.add)
                wa = dve("wtop", [ws], nc.vector.reciprocal, wtop[:, u, 0], wsum[:])
                wb = dve("wtop", [wa], nc.vector.tensor_tensor, wtop[:, u, 1], wexp[:], wtop[:, u, 0], ALU.mult)
                last_use["wexp"] = [wb]

            def count(banks):
                b0, b1 = banks
                flat = both[:].rearrange("p t n -> p (t n)")
                pe("rank", [seen["both"], *freed[b0]], nc.tensor.matmul,
                   bank[b0][:, 0:UT * E], before, flat, start=True, stop=True)
                mm = pe("rank", [ones_set, *freed[b1]], nc.tensor.matmul,
                        bank[b1][:, 0:UT * E], ones[:], flat, start=True, stop=True)
                wh = dve("whole", [mm], nc.vector.tensor_copy,
                         whole[:].rearrange("p t n -> p (t n)"), bank[b1][:, 0:UT * E])
                freed[b1] = [wh]
                rk = dve("rank", [mm], nc.vector.tensor_copy,
                         rank[:].rearrange("p t n -> p (t n)"), bank[b0][:, 0:UT * E])
                freed[b0] = [rk]
                for n in range(E):
                    seen["upto"] = dve("upto", [wh], nc.vector.tensor_tensor_scan,
                                       upto[:, :, n], ones[:, 0:UT], whole[:, :, n], 0.0, ALU.mult, ALU.add)
                last_use["fxn"] = [mm]

            def place(banks):
                up = seen["upto"]
                r1 = dve("rank", [up], nc.vector.tensor_tensor, rank[:], rank[:], upto[:], ALU.add)
                r2 = dve("rank", [r1], nc.vector.tensor_tensor, rank[:], rank[:], whole[:], ALU.subtract)
                n1 = dve("tiles", [up], nc.vector.tensor_scalar,
                         n_int[:, 0], upto[:, UT - 1, :], P - 1.0, None, ALU.add)
                n2 = dve("tiles", [n1], nc.vector.tensor_scalar,
                         n_int[:, 1], n_int[:, 0], P.bit_length() - 1, None, ALU.logical_shift_right)
                n3 = dve("tiles", [n2], nc.vector.tensor_copy, n_flt[:, 0], n_int[:, 1])
                n4 = dve("tiles", [n3], nc.vector.tensor_tensor_scan,
                         n_flt[:, 1], ones[:, 0:E], n_flt[:, 0], 0.0, ALU.mult, ALU.add)
                n5 = dve("tiles", [n4], nc.vector.tensor_tensor, n_flt[:, 2], n_flt[:, 1], n_flt[:, 0], ALU.subtract)
                r3 = dve("rank", [r2, n5], nc.vector.scalar_tensor_tensor,
                         out=rank[:], in0=n_flt[:, 2:3, :].broadcast_to([P, UT, E]), scalar=float(P), in1=rank[:],
                         op0=ALU.mult, op1=ALU.add)
                sl = None
                for i in range(TOP):
                    own = dve("slot", [r3, sl], nc.vector.tensor_tensor, hit[:], hot[:, i], rank[:], ALU.mult)
                    sl = dve("slot", [own], nc.vector.reduce_sum, slot_f[:, i, :], hit[:], AX_X)
                placed = dve("placed", [sl, *last_use["slot"][u]], nc.vector.tensor_copy, slot[:, u], slot_f[:])
                o1 = dve("owner", [n4], nc.vector.tensor_tensor,
                         passed[:], iota_s[0:1, :].rearrange("p (s o) -> p s o", o=1).broadcast_to([1, ST, E]),
                         n_flt[0:1, 1:2, :].broadcast_to([1, ST, E]), ALU.is_ge)
                o2 = dve("owner", [o1], nc.vector.reduce_sum, owner_f[:, 0, :], passed[:], AX_X)
                o3 = dve("owner", [o2], nc.vector.tensor_scalar,
                         owner_f[:, 1, :], owner_f[:, 0, :], E - 1.0, float(F), ALU.min, ALU.mult)
                owned = dve("owner", [o3, *last_use["owner"][u]], nc.vector.tensor_copy, owner[:, u, :], owner_f[:, 1, :])
                routed[u] = (normed, placed, owned)

            steps = [step for n in range(B // U) for step in norm_to_fxn(n)]
            steps.append(turn(0))
            for c in range(1, UT // 4):
                steps += [turn(c), gates(c - 1)]
            return [*steps, gates(UT // 4 - 1), weigh, count, place]

        def scatter(l, u):
            normed, placed, _ = routed[u]
            scattered[u] = []
            for t in range(UT):
                for i in range(TOP):
                    scattered[u].append(Q.add(
                        "gpsimd", f"scatter{l}{u}", [normed[-1], placed, *zeroed[u], *xs_read[u]], 16,
                        nc.gpsimd.indirect_dma_start, xs_dram[u],
                        bass.IndirectOffsetOnAxis(slot[:, u, i, t:t + 1], 0), fxn[:, t, :], None))
            last_use["fxn"] = scattered[u]

        def experts(l, u, steps, within):
            owned = routed[u][2]
            xs_tiles = xs_dram[u].rearrange("(n p) c -> p n c", p=P)
            ys_tiles = ys_dram[u].rearrange("(n p) c -> p n c", p=P)
            w1_flat = w1_sb[:].rearrange("c e f -> c (e f)")
            w2_flat = w2_sb[:].rearrange("f e k c -> f (e k c)")
            loaded, turned, hidden, weights = {}, {}, {}, {}

            def load(n):
                loaded[n] = Q.add("sync", f"xs{n % 2}", [*scattered[u], *last_use["xs"][n % 2]], 16,
                                  nc.sync.dma_start, xs[:, n % 2, :, :], xs_tiles[:, n * LOT:(n + 1) * LOT, :])

            def turn(n):
                if n % LOT == 0 and n // LOT + 1 < ST // LOT:
                    load(n // LOT + 1)
                lot, r = n // LOT, n % 2
                tr = pe("xsT", [loaded[lot], *freed[r]], nc.tensor.transpose,
                        bank[r][:, 0:P], xs[:, lot % 2, n % LOT, :], eye)
                last_use["xs"][lot % 2] = [tr]
                turned[n] = act("xsT", [tr, *last_use["xsT"][r]], nc.scalar.copy, xsT[:, r, :], bank[r][:, 0:P])
                freed[r] = [turned[n]]

            def own_weights(n, which, own, table, landed):
                r = n % 2

                def copy(to):
                    offset = nc.vector.value_load(owner[0:1, u, n:n + 1], min_val=0, max_val=(E - 1) * F)
                    return nc.vector.tensor_copy(to, table[:, bass.DynSlice(offset, F)])

                weights[which, n] = dve(which, [owned, landed, *last_use[which][r]], copy, own[:, r, :])
                last_use["owner"][u] = [weights[which, n]]

            def first(n):
                r = n % 2
                for k in range(FC):
                    mm = pe("first", [turned[n], weights["w1_own", n], *freed[2 + r]], nc.tensor.matmul,
                            bank[2 + r][:, k * P:(k + 1) * P], w1_own[:, r, k * P:(k + 1) * P], xsT[:, r, :],
                            start=k == 0, stop=k == FC - 1, skip_group_check=True)
                last_use["w1_own"][r] = [mm]
                last_use["xsT"][r] = [mm]
                hidden[n] = act("gelu", [mm, *last_use["hidT"][r]], nc.scalar.activation,
                                hidT[:, r, :], bank[2 + r][:], ACT.Gelu)
                freed[2 + r] = [hidden[n]]

            def second(n):
                lot, r = n // LOT, n % 2

                for k in range(FC):
                    mm = pe("second", [hidden[n], weights["w2_own", n], *freed[4 + r]], nc.tensor.matmul,
                            bank[4 + r][:, 0:C], hidT[:, r, k * P:(k + 1) * P], w2_own[:, r, k * C:(k + 1) * C],
                            start=k == 0, stop=k == FC - 1)
                last_use["w2_own"][r] = [mm]
                last_use["hidT"][r] = [mm]
                yd = dve("ys", [mm, *last_use["ys"][lot % 2]], nc.vector.tensor_copy,
                         ys[:, lot % 2, n % LOT, :], bank[4 + r][:, 0:C])
                freed[4 + r] = [yd]
                if n % LOT == LOT - 1:
                    st = Q.add("sync", f"ys{lot % 2}", [yd, *ys_read[u]], 16, nc.sync.dma_start,
                               ys_tiles[:, lot * LOT:(lot + 1) * LOT, :], ys[:, lot % 2, :, :])
                    last_use["ys"][lot % 2] = [st]
                    stored[u].append(st)

            stored[u] = []
            beside = ("xs", "xsT", "w1_own", "w2_own", "hidT")
            for name in beside:
                last_use[name] = [last_use[name][r] + last_use["pt"][0] + last_use["pt"][1] for r in range(2)]
            load(0)
            n_steps = len(steps)
            for n in range(ST + 2):
                while steps and n_steps - len(steps) < n_steps * (n - 1) / within:
                    steps.pop(0)((6, 7))
                if n < ST:
                    turn(n)
                    own_weights(n, "w1_own", w1_own, w1_flat, got_w1)
                if 0 <= n - 1 < ST:
                    own_weights(n - 1, "w2_own", w2_own, w2_flat, got_w2)
                    first(n - 1)
                if 0 <= n - 2 < ST:
                    second(n - 2)
            xs_read[u] = list(loaded.values())
            last_use["pt"] = [[token for name in beside for uses in last_use[name] for token in uses]] * 2

        def combine(l, u):
            fetched = {}

            def fetch(t):
                r = t % 4
                fetched[t] = [Q.add("gpsimd", f"got{r}", [*stored[u], *last_use["got"][r]], 16,
                                    nc.gpsimd.indirect_dma_start, got[:, r, i, :], None, ys_dram[u],
                                    bass.IndirectOffsetOnAxis(slot[:, u, i, t:t + 1], 0)) for i in range(TOP)]
                last_use["slot"][u] = ys_read[u] = fetched[t]

            def step(t):
                if t + 3 < UT:
                    fetch(t + 3)
                at, prev = u * UT + t, None
                for i in range(TOP):
                    prev = dve("moe", [*fetched[t], prev], nc.vector.scalar_tensor_tensor,
                               out=x[:, at, :], in0=got[:, t % 4, i, :], scalar=wtop[:, u, i, t],
                               in1=x[:, at, :], op0=ALU.mult, op1=ALU.add)
                last_use["got"][t % 4] = [prev]
                x_ready[at // TB] = [prev]
                if l == 1 and t % 4 == 3:
                    b, tb = at // TB, at % TB
                    stores.append(Q.add("sync", "store", [prev], 16, nc.sync.dma_start,
                                        out_dram[b][:, tb - 3:tb + 1, :], x[:, at - 3:at + 1, :]))

            return [lambda banks, t=t: fetch(t) for t in range(3)] + [lambda banks, t=t: step(t) for t in range(UT)]

        alongside = {t: [] for t in range(-1, TB)}

        def beside(t, banks):
            while alongside[t]:
                alongside[t].pop(0)(banks)

        def plan(first, steps, each=1):
            for i, step in enumerate(steps):
                alongside[first + i // each].append(step)

        prepared, routed, scattered, stored = {}, {}, {}, {}
        xs_read, ys_read = {u: [] for u in range(U)}, {u: [] for u in range(U)}
        stores = []

        def finish(steps):
            while steps:
                steps.pop(0)((6, 7))

        def plan_prepare(l, b, first=-1):
            moments_norm_turns = prepare(l, b)
            plan(first, moments_norm_turns[0:2])
            plan(min(first + 4, TB - 3), moments_norm_turns[2:])

        def plan_route(l, u):
            steps = route(l, u)
            heavy = 2 * B // U
            plan(-1, steps[:heavy])
            plan(2, steps[heavy:], 2)
            plan_prepare(l, B - 1, heavy - 1)

        finish(prepare(0, 0))
        plan_prepare(0, 1)
        attention(0, 0)
        plan_prepare(0, 2)
        attention(0, 1)
        plan_route(0, 0)
        attention(0, 2)
        plan(0, [lambda banks: scatter(0, 0)])
        attention(0, 3)
        experts(0, 0, route(0, 1) + [lambda banks: scatter(0, 1)], ST // 2)
        experts(0, 1, combine(0, 0) + prepare(1, 0), ST - 3)
        plan_prepare(1, 1)
        plan(0, combine(0, 1), 3)
        attention(1, 0)
        plan_prepare(1, 2)
        attention(1, 1)
        plan_route(1, 0)
        attention(1, 2)
        plan(0, [lambda banks: scatter(1, 0)])
        attention(1, 3)
        experts(1, 0, route(1, 1) + [lambda banks: scatter(1, 1)], ST // 2)
        experts(1, 1, combine(1, 0), ST - 3)
        finish(combine(1, 1))
        Q.add("sync", "end", stores, 1, nc.sync.drain)

        block = ctx.enter_context(nc.Block())
        Q.play(nc, ctx, block)


def kernel(**inputs):
    import concourse.bacc as bacc
    from concourse.bass_utils import run_bass_kernel_spmd

    a = {k: np.asarray(v) for k, v in inputs.items()}
    def heads(w):
        return w.reshape(*w.shape[:-1], G, J, D).swapaxes(-3, -2).reshape(w.shape)

    masks, picks, table = constants()
    pa, pb = "L0_attn_a_", "L0_attn_b_"
    b_cols = np.stack([heads(a[pb + n]) for n in ("bq", "bk")], axis=1)
    arrays = {
        "x_in": a[pa + "x"],
        "w_a": np.stack([heads(a[pa + n].T) for n in ("Wq", "Wk", "Wv")] + [heads(a[pa + "Wo"]).T]),
        "bo_a": a[pa + "bo"].reshape(1, C),
        "w_b": np.stack([heads(a[pb + n]) for n in ("Wq", "Wk", "Wv")] + [heads(a[pb + "Wo"].T).T]),
        "b_b": np.stack([heads(a[pb + n]) for n in ("bq", "bk", "bv")] + [a[pb + "bo"]]),
        "b_cols_in": b_cols,
        "gate_w": a["L0_ffn_gate_w"],
        "w1": a["L0_ffn_w1"],
        "w2": a["L0_ffn_w2"],
        "masks_in": masks,
        "picks_in": picks,
        "table_in": table,
    }
    nc = bacc.Bacc("TRN2", target_bir_lowering=False, num_devices=1)
    args = []
    for name, arr in arrays.items():
        arrays[name] = np.ascontiguousarray(arr)
        args.append(nc.dram_tensor(name, arr.shape, mybir.dt.from_np(arr.dtype), kind="ExternalInput").ap())
    args.append(nc.dram_tensor("out", (B, S, C), F32, kind="ExternalOutput").ap())
    build(nc, *args)
    return run_bass_kernel_spmd(nc, [arrays], core_ids=[0]).results[0]["out"]
```
